# Optimizing a Trainium2 kernel written in Bass

```python
import numpy as np
import jax
import jax.numpy as jnp

def _softmax(x, axis=-1):
    return jax.nn.softmax(x, axis=axis)

def _gelu(x):
    return jax.nn.gelu(x, approximate=True)

def _silu(x):
    return jax.nn.silu(x)

def _sigmoid(x):
    return jax.nn.sigmoid(x)

def _layernorm(x, axis=-1, eps=1e-05):
    m = jnp.mean(x, axis=axis, keepdims=True)
    v = jnp.var(x, axis=axis, keepdims=True)
    return (x - m) / jnp.sqrt(v + eps)

def _scatter_add(tgt, idx, src, axis=0):
    return tgt.at[idx].add(src)

def _segment_sum(src, seg, n):
    return jax.ops.segment_sum(src, seg, n)
kernel_name = 'mk_seq_preln_d2_jaxref_r4_c6df79'

def setup_inputs(seed: int=0):
    np.random.seed(seed)
    _w = jnp.asarray

    def _L0_attn_setup():
        import jax, jax.numpy as jnp
        import numpy as np
        D_MODEL, N_HEADS, BATCH, SEQ = (256, 16, 2, 512)

        def get_freqs(seq, n_dim):
            inv_freq = 1.0 / 10000.0 ** (jnp.arange(0, n_dim, 2, dtype=jnp.float32) / n_dim)
            pos = jnp.arange(seq, dtype=jnp.float32)
            return pos[:, None] * inv_freq[None, :]

        def rope(x, freq):
            cos = jnp.cos(freq)[None, :, None, :]
            sin = jnp.sin(freq)[None, :, None, :]
            x1, x2 = (x[..., ::2], x[..., 1::2])
            r1 = x1 * cos - x2 * sin
            r2 = x1 * sin + x2 * cos
            return jnp.stack([r1, r2], axis=-1).reshape(x.shape)
        key = jax.random.key(seed)
        ks = jax.random.split(key, 5)
        w_scale = 0.01
        return {'x': jax.random.normal(ks[0], (BATCH, SEQ, D_MODEL), dtype=jnp.float32), 'qw': jax.random.normal(ks[1], (D_MODEL, D_MODEL), dtype=jnp.float32) * w_scale, 'kw': jax.random.normal(ks[2], (D_MODEL, D_MODEL), dtype=jnp.float32) * w_scale, 'vw': jax.random.normal(ks[3], (D_MODEL, D_MODEL), dtype=jnp.float32) * w_scale, 'ow': jax.random.normal(ks[4], (D_MODEL, D_MODEL), dtype=jnp.float32) * w_scale}
    _L0_attn_in = _L0_attn_setup()

    def _L0_ffn_setup():
        import jax, jax.numpy as jnp
        import numpy as np
        DIM = 256
        HIDDEN = 768
        SCALE = 1.0 / 127.0

        def _dequant(w_int, dtype):
            return w_int.astype(dtype) * jnp.asarray(SCALE, dtype)
        key = jax.random.key(seed)
        k_x, k_g, k_u, k_d = jax.random.split(key, 4)
        x = jax.random.normal(k_x, (4, 512, DIM), dtype=jnp.float32)
        w_gate = jax.random.randint(k_g, (HIDDEN, DIM), -127, 128, dtype=jnp.int32)
        w_up = jax.random.randint(k_u, (HIDDEN, DIM), -127, 128, dtype=jnp.int32)
        w_down = jax.random.randint(k_d, (DIM, HIDDEN), -127, 128, dtype=jnp.int32)
        return {'x': x, 'w_gate': w_gate, 'w_up': w_up, 'w_down': w_down}
    _L0_ffn_in = _L0_ffn_setup()

    def _L1_attn_setup():
        import jax, jax.numpy as jnp
        import numpy as np
        OUT_DIM = 256
        key = jax.random.key(seed)
        k1, k2, k3, k4 = jax.random.split(key, 4)
        B, N, D = (4, 512, 256)
        s = 1.0 / np.sqrt(D)
        return {'x': jax.random.normal(k1, (B, N, D), dtype=jnp.float32), 'W_query': jax.random.normal(k2, (D, OUT_DIM), dtype=jnp.float32) * s, 'W_key': jax.random.normal(k3, (D, OUT_DIM), dtype=jnp.float32) * s, 'W_value': jax.random.normal(k4, (D, OUT_DIM), dtype=jnp.float32) * s}
    _L1_attn_in = _L1_attn_setup()

    def _L1_ffn_setup():
        import jax, jax.numpy as jnp
        import numpy as np
        B, S, D = (2, 512, 256)
        E, K, F = (16, 2, 128)
        FS = 256
        key = jax.random.key(seed)
        ks = jax.random.split(key, 8)

        def w(k, shape, fan_in):
            return jax.random.normal(k, shape, jnp.float32) / np.sqrt(fan_in).astype(np.float32)
        return {'x': jax.random.normal(ks[0], (B, S, D), jnp.float32), 'Wr': w(ks[1], (D, E), D), 'Wg': w(ks[2], (E, D, F), D), 'Wu': w(ks[3], (E, D, F), D), 'Wd': w(ks[4], (E, F, D), F), 'Sg': w(ks[5], (D, FS), D), 'Su': w(ks[6], (D, FS), D), 'Sd': w(ks[7], (FS, D), FS)}
    _L1_ffn_in = _L1_ffn_setup()
    _d = {'L0_attn_x': _L0_attn_in['x'], 'L0_attn_qw': _L0_attn_in['qw'], 'L0_attn_kw': _L0_attn_in['kw'], 'L0_attn_vw': _L0_attn_in['vw'], 'L0_attn_ow': _L0_attn_in['ow'], 'L0_ffn_w_gate': _L0_ffn_in['w_gate'], 'L0_ffn_w_up': _L0_ffn_in['w_up'], 'L0_ffn_w_down': _L0_ffn_in['w_down'], 'L1_attn_W_query': _L1_attn_in['W_query'], 'L1_attn_W_key': _L1_attn_in['W_key'], 'L1_attn_W_value': _L1_attn_in['W_value'], 'L1_ffn_Wr': _L1_ffn_in['Wr'], 'L1_ffn_Wg': _L1_ffn_in['Wg'], 'L1_ffn_Wu': _L1_ffn_in['Wu'], 'L1_ffn_Wd': _L1_ffn_in['Wd'], 'L1_ffn_Sg': _L1_ffn_in['Sg'], 'L1_ffn_Su': _L1_ffn_in['Su'], 'L1_ffn_Sd': _L1_ffn_in['Sd']}
    _x0 = _d['L0_attn_x']
    _d['L0_attn_x'] = jax.random.normal(jax.random.fold_in(jax.random.key(seed), 1), (8, 1024, 256), dtype=_x0.dtype)
    del _x0
    return _d

def reference(L0_attn_x, L0_attn_qw, L0_attn_kw, L0_attn_vw, L0_attn_ow, L0_ffn_w_gate, L0_ffn_w_up, L0_ffn_w_down, L1_attn_W_query, L1_attn_W_key, L1_attn_W_value, L1_ffn_Wr, L1_ffn_Wg, L1_ffn_Wu, L1_ffn_Wd, L1_ffn_Sg, L1_ffn_Su, L1_ffn_Sd):

    def _L0_attn_ref(x, qw, kw, vw, ow):
        import jax, jax.numpy as jnp
        import numpy as np
        D_MODEL, N_HEADS, BATCH, SEQ = (256, 16, 2, 512)

        def get_freqs(seq, n_dim):
            inv_freq = 1.0 / 10000.0 ** (jnp.arange(0, n_dim, 2, dtype=jnp.float32) / n_dim)
            pos = jnp.arange(seq, dtype=jnp.float32)
            return pos[:, None] * inv_freq[None, :]

        def rope(x, freq):
            cos = jnp.cos(freq)[None, :, None, :]
            sin = jnp.sin(freq)[None, :, None, :]
            x1, x2 = (x[..., ::2], x[..., 1::2])
            r1 = x1 * cos - x2 * sin
            r2 = x1 * sin + x2 * cos
            return jnp.stack([r1, r2], axis=-1).reshape(x.shape)
        batch, seq, dim = x.shape
        n_heads = N_HEADS
        n_dim = dim // n_heads
        Q = (x @ qw).astype(jnp.float32).reshape(batch, seq, n_heads, n_dim)
        K = (x @ kw).astype(jnp.float32).reshape(batch, seq, n_heads, n_dim)
        V = (x @ vw).astype(jnp.float32).reshape(batch, seq, n_heads, n_dim)
        freq = get_freqs(seq, n_dim)
        Q = rope(Q, freq)
        K = rope(K, freq)
        Q = jnp.transpose(Q, (0, 2, 1, 3))
        K = jnp.transpose(K, (0, 2, 1, 3))
        V = jnp.transpose(V, (0, 2, 1, 3))
        scale = jnp.sqrt(jnp.float32(n_dim))
        score = jnp.einsum('bhqd,bhkd->bhqk', Q, K) / scale
        causal = jnp.tril(jnp.ones((1, 1, seq, seq), dtype=jnp.float32))
        score = score - 10000000000.0 * (1.0 - causal)
        score = score - jnp.max(score, axis=-1, keepdims=True)
        weights = jax.nn.softmax(score, axis=-1)
        attn = jnp.einsum('bhqk,bhkd->bhqd', weights, V)
        merged = jnp.transpose(attn, (0, 2, 1, 3)).reshape(batch, seq, dim)
        return (merged @ ow).astype(x.dtype)

    def _L0_ffn_ref(x, w_gate, w_up, w_down):
        import jax, jax.numpy as jnp
        import numpy as np
        DIM = 256
        HIDDEN = 768
        SCALE = 1.0 / 127.0

        def _dequant(w_int, dtype):
            return w_int.astype(dtype) * jnp.asarray(SCALE, dtype)
        wg = _dequant(w_gate, x.dtype)
        wu = _dequant(w_up, x.dtype)
        wd = _dequant(w_down, x.dtype)
        gate = jnp.einsum('bsd,hd->bsh', x, wg)
        up = jnp.einsum('bsd,hd->bsh', x, wu)
        h = jax.nn.silu(gate) * up
        return jnp.einsum('bsh,dh->bsd', h, wd)

    def _L1_attn_ref(x, W_query, W_key, W_value):
        import jax, jax.numpy as jnp
        import numpy as np
        OUT_DIM = 256
        q = jnp.einsum('bnd,de->bne', x, W_query)
        k = jnp.einsum('bnd,de->bne', x, W_key)
        v = jnp.einsum('bnd,de->bne', x, W_value)
        sqrt_d = jnp.sqrt(jnp.asarray(OUT_DIM, dtype=jnp.float32))
        scores = jnp.einsum('bie,bje->bij', q, k) / sqrt_d
        attn = jax.nn.softmax(scores, axis=1)
        return jnp.einsum('bij,bie->bje', attn, v)

    def _L1_ffn_ref(x, Wr, Wg, Wu, Wd, Sg, Su, Sd):
        import jax, jax.numpy as jnp
        import numpy as np
        B, S, D = (2, 512, 256)
        E, K, F = (16, 2, 128)
        FS = 256
        b, s, d = x.shape
        T = b * s
        xf = x.reshape(T, d)
        shared = jax.nn.silu(xf @ Sg) * (xf @ Su) @ Sd
        probs = jax.nn.softmax(xf @ Wr, axis=-1)
        topk_p, topk_i = jax.lax.top_k(probs, K)
        n_exp = Wr.shape[1]
        cw = jnp.zeros((T, n_exp), x.dtype).at[jnp.arange(T)[:, None], topk_i].add(topk_p)

        def step(acc, ew):
            wg, wu, wd, c = ew
            y = jax.nn.silu(xf @ wg) * (xf @ wu) @ wd
            return (acc + y * c[:, None], None)
        routed, _ = jax.lax.scan(step, jnp.zeros_like(xf), (Wg, Wu, Wd, cw.T))
        return (routed + shared).reshape(b, s, d)
    x = L0_attn_x
    x = x + _L0_attn_ref(_layernorm(x, axis=-1), L0_attn_qw, L0_attn_kw, L0_attn_vw, L0_attn_ow)
    x = x + _L0_ffn_ref(_layernorm(x, axis=-1), L0_ffn_w_gate, L0_ffn_w_up, L0_ffn_w_down)
    x = x + _L1_attn_ref(_layernorm(x, axis=-1), L1_attn_W_query, L1_attn_W_key, L1_attn_W_value)
    x = x + _L1_ffn_ref(_layernorm(x, axis=-1), L1_ffn_Wr, L1_ffn_Wg, L1_ffn_Wu, L1_ffn_Wd, L1_ffn_Sg, L1_ffn_Su, L1_ffn_Sd)
    return x

_drawn_inputs = setup_inputs


def setup_inputs(seed=0):
    import zlib

    import numpy as np

    out = dict(_drawn_inputs(seed))
    spreads = {}
    factors = {'L0_attn_qw': 8.0,
     'L0_attn_kw': 8.0,
     'L0_attn_vw': 8.0,
     'L0_attn_ow': 8.0,
     'L1_attn_W_query': 37.369,
     'L1_attn_W_key': 38.878,
     'L1_attn_W_value': 37.748,
     'L1_ffn_Wr': 8.0,
     'L1_ffn_Wg': 8.0,
     'L1_ffn_Wu': 8.0,
     'L1_ffn_Wd': 8.0,
     'L1_ffn_Sg': 8.0,
     'L1_ffn_Su': 8.0,
     'L1_ffn_Sd': 8.0}
    for name, (base, spread) in spreads.items():
        noise = np.random.default_rng([zlib.crc32(name.encode()), seed]).standard_normal(out[name].shape)
        drawn = base * np.exp(spread * noise) if base else spread * noise
        out[name] = jnp.asarray(drawn.astype(out[name].dtype))
    for name, factor in factors.items():
        out[name] = (out[name] * factor).astype(out[name].dtype)
    return out
```

```python
from contextlib import ExitStack

import numpy as np

import concourse.bass as bass
from concourse import mybir

F32 = mybir.dt.float32
F32R = mybir.dt.float32r
BF16 = mybir.dt.bfloat16
I32 = mybir.dt.int32
U32 = mybir.dt.uint32
ACT = mybir.ActivationFunctionType
ALU = mybir.AluOpType
AX_X = mybir.AxisListType.X

P = 128
BATCH, SEQ, D = 8, 1024, 256
TOKENS = BATCH * SEQ
KC = D // P
GT = 4
GN = GT * P
GROUPS = TOKENS // GN
EPS = 1e-5
NEWTON = 3
ROOT_STEPS = 2 + 3 * NEWTON


def at_least(engine, semaphore, value):
    if not (isinstance(value, int) and value <= 0):
        engine.wait_ge(semaphore, value)


def waits_apart(engine, *waits):
    waits = [(s, v if isinstance(v, int) else engine.to_reg(v)) for s, v in waits]
    if not isinstance(waits[-1][1], int):
        engine.wait_ge(waits[0][0], 1)
    for semaphore, value in waits:
        at_least(engine, semaphore, value)


def pipelined(engine, step, count, ways=2):
    for i in range(ways):
        step(i, i)
    with engine.Fori(1, count // ways - 1) as turn:
        for k in range(ways):
            step(ways * turn + k, k)
    for k in range(ways):
        step(count - ways + k, k)


def is_first(i):
    return isinstance(i, int) and i == 0


def is_last(i, count):
    return isinstance(i, int) and i == count - 1


def group_rows(x, g):
    return x[bass.ds(g * GN, GN), :].rearrange("(t p) d -> p t d", p=P)


def fill_identity(nc, identity, done):
    nc.gpsimd.memset(identity[:], 0.0).then_inc(done, 1)
    nc.gpsimd.wait_ge(done, 1)
    nc.gpsimd.affine_select(out=identity[:], in_=identity[:], compare_op=ALU.not_equal, fill=1.0, base=0,
                            pattern=[[-1, P]], channel_multiplier=1).then_inc(done, 1)


class Front:

    def __init__(self, nc, ctx, tag, turned):
        sb = lambda n, s, d: ctx.enter_context(nc.sbuf_tensor(f"{tag}_{n}", s, d))
        sem = lambda n: ctx.enter_context(nc.semaphore(f"{tag}_{n}"))
        self.nc = nc
        self.x = [sb(f"x{i}", [P, GT, D], F32) for i in range(2)]
        self.resid = [sb(f"resid{i}", [P, GT, D], F32) for i in range(2)]
        self.xn = sb("xn", [P, GT, D], F32)
        self.stats = sb("stats", [P, GT, 6], F32)
        self.moments = sb("moments", [P, GT, 2], F32)
        self.variance = sb("variance", [P, GT], F32)
        self.rstd = sb("rstd", [P, GT], F32)
        self.root_t = sb("root_t", [P, GT], F32)
        self.high = [sb(f"high{i}", [P, KC, GN], F32R) for i in range(2)]
        self.low = [sb(f"low{i}", [P, KC, GN], F32R) for i in range(2)]
        self.turned = turned
        self.x_loaded = [sem("x_loaded_even"), sem("x_loaded_odd")]
        self.stats_done = sem("stats_done")
        self.xn_ready = sem("xn_ready")
        self.turned_ready = sem("turned_ready")
        self.high_ready = sem("high_ready")
        self.low_ready = sem("low_ready")

    def load(self, x_in, g, slot):
        at_least(self.nc.sync, self.xn_ready, g - 1)
        self.nc.sync.dma_start(self.x[slot][:], group_rows(x_in, g)).then_inc(self.x_loaded[slot], 16)

    def normalise(self, g, slot, resid_free=(), keep=True):
        dve, x = self.nc.vector, self.x[slot]
        steps = 2 * GT + ROOT_STEPS
        dve.wait_ge(self.x_loaded[slot], 8 * g + 16 - 8 * slot)
        for t in range(GT):
            dve.bn_stats(self.stats[:, t, :], x[:, t, :]).then_inc(self.stats_done, 1)
        for semaphore, value in resid_free:
            at_least(dve, semaphore, value)
        if keep:
            dve.tensor_copy(self.resid[slot][:], x[:])
        waits_apart(dve, (self.stats_done, steps * g + GT))
        for t in range(GT):
            dve.bn_aggr(self.moments[:, t, :], self.stats[:, t, :]).then_inc(self.stats_done, 1)
        dve.wait_ge(self.stats_done, steps * g + 2 * GT)
        self.inverse_root(steps * g + 2 * GT)
        at_least(dve, self.turned_ready, g)
        for t in range(GT):
            ins = dve.tensor_scalar(self.xn[:, t, :], x[:, t, :], self.moments[:, t, 0:1], self.rstd[:, t:t + 1],
                                    ALU.subtract, ALU.mult)
        ins.then_inc(self.xn_ready, 1)

    def inverse_root(self, done):
        dve, v, y, t = self.nc.vector, self.variance, self.rstd, self.root_t
        ops = [lambda: dve.tensor_scalar(v[:], self.moments[:, :, 1], EPS, None, ALU.add),
               lambda: dve.tensor_scalar(y[:].bitcast(I32), v[:].bitcast(I32), -0.5, float(0x5F3759DF), ALU.mult, ALU.add)]
        for _ in range(NEWTON):
            ops += [lambda: dve.tensor_tensor(t[:], y[:], y[:], ALU.mult),
                    lambda: dve.scalar_tensor_tensor(t[:], t[:], -0.5, v[:], ALU.mult, ALU.mult),
                    lambda: dve.scalar_tensor_tensor(y[:], t[:], 1.5, y[:], ALU.add, ALU.mult)]
        for n, op in enumerate(ops):
            op().then_inc(self.stats_done, 1)
            dve.wait_ge(self.stats_done, done + n + 1)

    def turn(self, g, identity):
        pe = self.nc.tensor
        pe.wait_ge(self.xn_ready, g + 1)
        at_least(pe, self.low_ready, g)
        for c in range(KC):
            for t in range(GT):
                ins = pe.transpose(self.turned[:, c, t * P:(t + 1) * P], self.xn[:, t, c * P:(c + 1) * P], identity)
        ins.then_inc(self.turned_ready, 1)

    def take_high(self, g, slot):
        self.nc.scalar.wait_ge(self.turned_ready, g + 1)
        self.nc.scalar.copy(self.high[slot][:], self.turned[:]).then_inc(self.high_ready, 1)

    def take_low(self, g, slot):
        dve = self.nc.vector
        dve.wait_ge(self.high_ready, g + 1)
        dve.tensor_tensor(self.low[slot][:], self.turned[:], self.high[slot][:].bitcast(F32),
                          ALU.subtract).then_inc(self.low_ready, 1)


def product(nc, out, pairs, start=True, stop=True, shared=False):
    n = 0
    for wh, wl, mh, ml in pairs:
        for w, m in ((wh, mh), (wl, mh), (wh, ml)):
            ins = nc.tensor.matmul(out, w, m, start=start and n == 0, stop=stop and n == 3 * len(pairs) - 1,
                                   skip_group_check=shared)
            n += 1
    return ins
HEADS = 16
HD = D // HEADS
HALF = HD // 2
HG = 4
UNITS = BATCH * HEADS // HG
PARTS = 3
QK = 2
VW = 32
QBLOCKS = SEQ // P
TILES = TOKENS // P


def rope_qkv(nc, x_in, w_qkv, cos, sin, qk_out, v_out):
    with ExitStack() as ctx:
        sb = lambda n, s, d: ctx.enter_context(nc.sbuf_tensor(f"qkv_{n}", s, d))
        ps = lambda n, s, d=F32: ctx.enter_context(nc.psum_tensor(f"qkv_{n}", s, d))
        sem = lambda n: ctx.enter_context(nc.semaphore(f"qkv_{n}"))
        W = KC * 3 * D
        w_f = sb("w_f", [P, W], F32)
        w_high = sb("w_high", [P, W], F32R)
        w_low = sb("w_low", [P, W], F32R)
        identity = sb("identity", [P, P], F32)
        identity16 = sb("identity16", [P, P], BF16)
        cos_t = sb("cos", [P, QBLOCKS, HALF], F32)
        sin_t = sb("sin", [P, QBLOCKS, 2, HALF], F32)
        RING = GT
        by_cos = [sb(f"by_cos{i}", [P, QK * D], F32) for i in range(2)]
        by_sin = [sb(f"by_sin{i}", [P, QK * D], F32) for i in range(2)]
        r = [sb(f"r{i}", [P, QK * D], F32) for i in range(RING)]
        rest = [sb(f"rest{i}", [P, QK * D], F32) for i in range(RING)]
        parts = [sb(f"parts{i}", [P, PARTS, QK * D], BF16) for i in range(RING)]
        stage = [sb(f"stage{i}", [P, QK * PARTS, KC, GN], BF16) for i in range(2)]
        v_stage = [sb(f"v_stage{i}", [P, GT, HEADS, VW], F32) for i in range(2)]
        turned = ps("turned", [P, KC, GN])
        qk = [ps(f"qk{i}", [P, QK * D]) for i in range(2)]
        v = [ps(f"v{i}", [P, D]) for i in range(2)]
        across = [ps(f"across{i}", [P, PARTS * KC, P], BF16) for i in range(QK)]
        f = Front(nc, ctx, "qkv", turned)
        w_loaded, w_ready, consts = sem("w_loaded"), sem("w_ready"), sem("consts")
        qk_ready, v_ready = sem("qk_ready"), sem("v_ready")
        rope_ready = sem("rope_ready")
        r_ready, rest_ready = sem("r_ready"), sem("rest_ready")
        v_taken, first_ready, second_ready = sem("v_taken"), sem("first_ready"), sem("second_ready")
        third_ready = sem("third_ready")
        across_ready = sem("across_ready")
        q_taken, k_taken = sem("q_taken"), sem("k_taken")
        stored = [sem("stored_even"), sem("stored_odd")]
        v_stored = [sem("v_stored_even"), sem("v_stored_odd")]
        STORES = HEADS // HG

        block = ctx.enter_context(nc.Block())

        def lagged(n, lag):
            return not isinstance(n, int) or 0 <= n - lag < TILES

        @block.sync
        def _(sp):
            sp.dma_start(w_f[:].rearrange("p (c n) -> p c n", c=KC), w_qkv.rearrange("(c p) n -> p c n", p=P)).then_inc(w_loaded, 16)
            sp.dma_start(cos_t[:], cos.rearrange("(t p) e -> p t e", p=P)).then_inc(w_loaded, 16)
            sp.dma_start(sin_t[:], sin.rearrange("(t p) (s e) -> p t s e", p=P, s=2)).then_inc(w_loaded, 16)
            f.load(x_in, 0, 0)
            f.load(x_in, 1, 1)

            def store_qk(g, slot, b):
                sp.wait_ge(q_taken, GT * (g + 1))
                sp.wait_ge(k_taken, GT * (g + 1))
                for side in range(2):
                    for c in range(KC):
                        out = qk_out[bass.ds(b * (HEADS // HG) + 2 * c + side, 1), :, :, slot * GN:(slot + 1) * GN]
                        sp.dma_start(out.rearrange("u a p n -> p (u a) n"),
                                     stage[slot][64 * side:64 * side + 64, :, c, :]).then_inc(stored[slot], 16)

            def store_v(g, slot, b):
                sp.wait_ge(v_taken, GT * (g + 1))
                for unit in range(HEADS // HG):
                    out = v_out[bass.ds(b * (HEADS // HG) + unit, 1), slot * GN:(slot + 1) * GN, :]
                    sp.dma_start(out.rearrange("u (t p) n -> p (u t) n", p=P),
                                 v_stage[slot][:, :, unit * HG:(unit + 1) * HG, :].rearrange("p t h n -> p t (h n)")).then_inc(v_stored[slot], 16)

            def pair(b):
                if not is_last(b, BATCH):
                    f.load(x_in, 2 * b + 2, 0)
                if not is_first(b):
                    store_qk(2 * b - 1, 1, b - 1)
                store_v(2 * b, 0, b)
                if not is_last(b, BATCH):
                    f.load(x_in, 2 * b + 3, 1)
                store_qk(2 * b, 0, b)
                store_v(2 * b + 1, 1, b)
            pair(0)
            with sp.Fori(1, BATCH - 1) as b:
                pair(b)
            pair(BATCH - 1)
            store_qk(GROUPS - 1, 1, BATCH - 1)
            for s in stored + v_stored:
                sp.wait_ge(s, 16 * STORES * GROUPS // 2)

        @block.gpsimd
        def _(pool):
            fill_identity(nc, identity, consts)
            pool.wait_ge(consts, 2)
            nc.gpsimd.tensor_copy(identity16[:], identity[:]).then_inc(consts, 1)
            for s in v_stage:
                nc.gpsimd.memset(s[:], 0.0).then_inc(consts, 1)
            pool.wait_ge(consts, 5)
            for s in v_stage:
                nc.gpsimd.memset(s[:, :, :, HD:HD + 1], 1.0).then_inc(consts, 1)

            def tile(n, t):
                if lagged(n, 0):
                    at_least(pool, first_ready, n - 3)
                    at_least(pool, rest_ready, n - 3)
                    pool.wait_ge(rope_ready, n + 1)
                    nc.gpsimd.tensor_tensor(r[t][:], by_cos[t % 2][:], by_sin[t % 2][:], ALU.add).then_inc(r_ready, 1)
                if lagged(n, 1):
                    s = (t - 1) % RING
                    at_least(pool, third_ready, n - 4)
                    pool.wait_ge(first_ready, n)
                    nc.gpsimd.tensor_tensor(rest[s][:], r[s][:], parts[s][:, 0, :], ALU.subtract).then_inc(rest_ready, 1)
            pipelined(pool, lambda g, slot: [tile(GT * g + t, t) for t in range(GT)], GROUPS)
            tile(TILES, 0)

        @block.scalar
        def _(act):
            f.take_high(0, 0)

            def tile(n, t, slot):
                if lagged(n, 4):
                    at = 1 - slot
                    act.wait_ge(across_ready, n - 3)
                    if t == 0:
                        at_least(act, stored[at], 2 * STORES * (n - 4) - 8 * STORES * at)
                    nc.scalar.copy(stage[at][:, 0:PARTS, :, t * P:(t + 1) * P],
                                   across[0][:].rearrange("p (a c) n -> p a c n", c=KC)).then_inc(q_taken, 1)
                if lagged(n, 0):
                    act.wait_ge(v_ready, n + 1)
                    if t == 0:
                        at_least(act, v_stored[slot], 2 * STORES * n - 8 * STORES * slot)
                        if isinstance(n, int) and n < 2 * GT:
                            act.wait_ge(consts, 7)
                    nc.scalar.copy(v_stage[slot][:, t, :, 0:HD], v[t % 2][:].rearrange("p (h e) -> p h e", h=HEADS)).then_inc(v_taken, 1)
                    at_least(act, across_ready, n - 3)
                    act.wait_ge(r_ready, n + 1)
                    nc.scalar.copy(parts[t][:, 0, :], r[t][:]).then_inc(first_ready, 1)
                if lagged(n, 1):
                    s = (t - 1) % RING
                    act.wait_ge(rest_ready, n)
                    nc.scalar.copy(parts[s][:, 1, :], rest[s][:]).then_inc(second_ready, 1)

            def step(g, slot):
                for t in range(GT):
                    if t == 2 and not is_last(g, GROUPS):
                        at_least(act, v_ready, GT * g)
                        f.take_high(g + 1, 1 - slot)
                    tile(GT * g + t, t, slot)
            pipelined(act, step, GROUPS)
            for t in range(4):
                tile(TILES + t, t, 0)

        @block.vector
        def _(dve):
            dve.wait_ge(w_loaded, 48)
            nc.vector.tensor_copy(w_high[:], w_f[:]).then_inc(w_ready, 1)
            dve.wait_ge(w_ready, 1)
            nc.vector.tensor_tensor(w_low[:], w_f[:], w_high[:].bitcast(F32), ALU.subtract).then_inc(w_ready, 1)
            f.normalise(0, 0)
            f.take_low(0, 0)

            def tile(n, t, slot):
                if lagged(n, 4):
                    at = 1 - slot
                    dve.wait_ge(across_ready, n - 3)
                    if t == 0:
                        at_least(dve, stored[at], 2 * STORES * (n - 4) - 8 * STORES * at)
                    nc.vector.tensor_copy(stage[at][:, PARTS:2 * PARTS, :, t * P:(t + 1) * P],
                                          across[1][:].rearrange("p (a c) n -> p a c n", c=KC)).then_inc(k_taken, 1)
                if lagged(n, 0):
                    where = slot * GT + t
                    dve.wait_ge(qk_ready, n + 1)
                    at_least(dve, r_ready, n - 1)
                    x = qk[t % 2][:].rearrange("p (h s e) -> p h s e", s=2, e=HALF)
                    c = cos_t[:, where:where + 1, :].broadcast_to([P, 2 * QK * HEADS, HALF])
                    nc.vector.tensor_tensor(by_cos[t % 2][:].rearrange("p (h e) -> p h e", e=HALF),
                                            qk[t % 2][:].rearrange("p (h e) -> p h e", e=HALF), c, ALU.mult)
                    out = by_sin[t % 2][:].rearrange("p (h s e) -> p h s e", s=2, e=HALF)
                    for s in range(2):
                        w = sin_t[:, where, s:s + 1, :].broadcast_to([P, QK * HEADS, HALF])
                        ins = nc.vector.tensor_tensor(out[:, :, s, :], x[:, :, 1 - s, :], w, ALU.mult)
                    ins.then_inc(rope_ready, 1)
                if lagged(n, 2):
                    s = (t - 2) % RING
                    dve.wait_ge(second_ready, n - 1)
                    nc.vector.tensor_tensor(parts[s][:, 2, :], rest[s][:], parts[s][:, 1, :], ALU.subtract).then_inc(third_ready, 1)

            def step(g, slot):
                for t in range(GT):
                    if t == 2 and not is_last(g, GROUPS):
                        f.take_low(g + 1, 1 - slot)
                    tile(GT * g + t, t, slot)
                    if t == 0 and not is_last(g, GROUPS):
                        f.normalise(g + 1, 1 - slot, keep=False)
            pipelined(dve, step, GROUPS)
            for t in range(4):
                tile(TILES + t, t, 0)

        @block.tensor
        def _(pe):
            pe.wait_ge(consts, 3)
            f.turn(0, identity[:])
            pe.wait_ge(w_ready, 2)

            def tile(n, t, slot):
                if lagged(n, 0):
                    at_least(pe, rope_ready, n - 1)
                    at_least(pe, v_taken, n - 1)
                    ts = slice(t * P, (t + 1) * P)
                    for bank, at, width, ready in ((qk, 0, QK * D, qk_ready), (v, QK * D, D, v_ready)):
                        cols = [slice(k * 3 * D + at, k * 3 * D + at + width) for k in range(KC)]
                        product(nc, bank[t % 2][:], [(f.high[slot][:, k, ts], f.low[slot][:, k, ts], w_high[:, cols[k]], w_low[:, cols[k]])
                                                     for k in range(KC)]).then_inc(ready, 1)
                if lagged(n, 3):
                    s = (t - 3) % RING
                    pe.wait_ge(third_ready, n - 2)
                    at_least(pe, q_taken, n - 3)
                    at_least(pe, k_taken, n - 3)
                    for i in range(QK):
                        for a in range(PARTS):
                            for c in range(KC):
                                ins = nc.tensor.transpose(across[i][:, a * KC + c, :], parts[s][:, a, i * D + c * P:i * D + (c + 1) * P], identity16[:])
                    ins.then_inc(across_ready, 1)

            def step(g, slot):
                pe.wait_ge(f.low_ready, g + 1)
                for t in range(GT):
                    tile(GT * g + t, t, slot)
                    if t == 1 and not is_last(g, GROUPS):
                        f.turn(g + 1, identity[:])
            pipelined(pe, step, GROUPS)
            for t in range(3):
                tile(TILES + t, t, 0)


STEPS = [(c, j) for c in range(2) for j in range(4 * c + 4)]
NSTEP = len(STEPS)
PIECES = [(i, lo) for i in range(QBLOCKS) for lo in range(0, (i + 1) * P, GN)]
NP_HEAD = len(PIECES)
NP_UNIT = HG * NP_HEAD
COMBOS = ((0, 0), (0, 1), (0, 2), (1, 0), (1, 1), (2, 0))
ROWS = len(COMBOS) * HD
LOW = -1e30
WAYS = 4
E_RING = 4
QUERY_SCALE = float(HD) ** -0.5


def causal_attention(nc, qk_in, v_in, o_out):
    with ExitStack() as ctx:
        sb = lambda n, s, d: ctx.enter_context(nc.sbuf_tensor(f"att_{n}", s, d))
        ps = lambda n, s, d=F32: ctx.enter_context(nc.psum_tensor(f"att_{n}", s, d))
        sem = lambda n: ctx.enter_context(nc.semaphore(f"att_{n}"))
        q = [sb(f"q{i}", [P, HG, SEQ], BF16) for i in range(WAYS)]
        k = [sb(f"k{i}", [P, HG, SEQ], BF16) for i in range(WAYS)]
        v = [sb(f"v{i}", [P, QBLOCKS, HG * VW], F32) for i in range(WAYS)]
        e = [sb(f"e{i}", [P, HG, GN], F32) for i in range(E_RING)]
        o = [sb(f"o{i}", [P, GN], F32) for i in range(2)]
        identity = sb("identity", [P, P], F32)
        identity16 = sb("identity16", [P, P], BF16)
        mask = sb("mask", [P, GN], F32)
        unused = [sb(f"unused{i}", [P, GN], F32) for i in range(3)]
        tops = sb("tops", [P, HG, QBLOCKS], F32)
        tops0 = sb("tops0", [P, HG, QBLOCKS // 2], F32)
        rest = sb("rest", [P, HG, QBLOCKS], F32)
        minus = sb("minus", [P, PARTS, HG, QBLOCKS], BF16)
        rows = sb("rows", [PARTS * HG * QBLOCKS, P], BF16)
        by_key = [ps(f"by_key{i}", [P, 2, GN]) for i in range(2)]
        by_query = [ps(f"by_query{i}", [P, GN]) for i in range(3)]
        total = ps("total", [P, GN])
        consts, loaded, v_loaded = sem("consts"), [sem(f"loaded{i}") for i in range(WAYS)], [sem(f"v_loaded{i}") for i in range(WAYS)]
        query_ready, query_read = sem("query_ready"), sem("query_read")
        split = sem("split")
        rows_turned, rows_taken, rows_placed = sem("rows_turned"), sem("rows_taken"), sem("rows_placed")
        key_ready, weights_ready = sem("key_ready"), sem("weights_ready")
        masked = sem("masked")
        summed = sem("summed")
        o_taken = sem("o_taken")
        o_stored = [sem("o_stored0"), sem("o_stored1")]
        SPLITS = 5
        LOADS = QK * len(COMBOS)
        DIAGONAL = 8
        AHEAD = 14
        TURN_AT = 3
        LAG = 3

        block = ctx.enter_context(nc.Block())

        def diagonal(s):
            c, j = STEPS[s]
            return j >= 4 * c

        def offset(s):
            c, j = STEPS[s]
            return max(0, j - 4 * c) * P

        def shares():
            parts = []
            for s in range(NSTEP):
                w = (s - LAG) % NSTEP
                parts += [2 * (GN - offset(s)) + 128, 2 * (GN - offset(s)) + 128, 5 * (GN - offset(w)) // 2 + 128]
            order = [m % NP_UNIT for m in range(AHEAD, AHEAD + NP_UNIT)]
            costs = [min((i + 1) * P - lo, GN) + 128 for i, lo in (PIECES[m % NP_HEAD] for m in order)]
            share, n = [0], 0
            for k in range(len(parts)):
                while n < NP_UNIT and sum(costs[:n]) * sum(parts) < sum(parts[:k + 1]) * sum(costs):
                    n += 1
                share.append(n)
            return share

        SHARE = shares()

        def diagonals_to(s):
            return sum(diagonal(i) for i in range(s + 1))

        @block.sync
        def _(sp):
            def load(u, way):
                for i, stack in enumerate((q, k)):
                    for n, combo in enumerate(COMBOS):
                        a = i * PARTS + combo[i]
                        src = qk_in[bass.ds(u, 1), a, :, :].rearrange("u (j d) n -> d (u j) n", d=HD)
                        sp.dma_start(stack[way][n * HD:(n + 1) * HD, :, :], src).then_inc(loaded[way], 16)
                sp.dma_start(v[way][:], v_in[bass.ds(u, 1), :, :].rearrange("u (t p) n -> p (u t) n", p=P)).then_inc(v_loaded[way], 16)

            def place(u, way):
                sp.wait_ge(rows_taken, u + 1)
                n = HG * QBLOCKS
                for a in range(PARTS):
                    sp.dma_start(q[way][ROWS + a:ROWS + a + 1, :, :].rearrange("a j (i n) -> a (j i) n", n=P),
                                 rows[a * n:(a + 1) * n, :]).then_inc(rows_placed, 16)

            def store(u, c):
                sp.wait_ge(o_taken, 2 * u + c + 1)
                sp.dma_start(o_out[bass.ds(u, 1), :, c * GN:(c + 1) * GN].rearrange("u p n -> p (u n)"), o[c][:]).then_inc(o_stored[c], 16)
            load(0, 0)
            load(1, 1)
            load(2, 2)
            place(0, 0)

            def step(u, way):
                if not is_first(u):
                    store(u - 1, 1)
                if not (isinstance(u, int) and u + 3 >= UNITS):
                    at_least(sp, summed, NSTEP * u)
                    load(u + 3, (way + 3) % WAYS)
                store(u, 0)
                if not is_last(u, UNITS):
                    place(u + 1, (way + 1) % WAYS)
            pipelined(sp, step, UNITS, WAYS)
            store(UNITS - 1, 1)
            for s in o_stored:
                sp.wait_ge(s, 16 * UNITS)

        @block.gpsimd
        def _(pool):
            fill_identity(nc, identity, consts)
            pool.wait_ge(consts, 2)
            nc.gpsimd.tensor_copy(identity16[:], identity[:]).then_inc(consts, 1)
            nc.gpsimd.memset(mask[:], 0.0).then_inc(consts, 1)
            pool.wait_ge(consts, 4)
            last = mask[:, GN - P:GN]
            nc.gpsimd.affine_select(out=last, in_=last, compare_op=ALU.is_ge, fill=LOW, base=0,
                                    pattern=[[-1, P]], channel_multiplier=1).then_inc(consts, 1)
            for i, s in enumerate(k):
                pool.wait_ge(consts, 5 + i)
                nc.gpsimd.memset(s[ROWS:P, :, :], 1.0).then_inc(consts, 1)

            def step(u, way):
                for s in range(NSTEP):
                    if diagonal(s):
                        waits_apart(pool, (weights_ready, 2 * (NSTEP * u + s + 1)))
                        w = e[s % E_RING][:, :, offset(s):offset(s) + P]
                        nc.gpsimd.affine_select(out=w, in_=w, compare_op=ALU.is_ge, fill=0.0, base=0,
                                                pattern=[[0, HG], [1, P]], channel_multiplier=-1).then_inc(masked, 1)
            pipelined(pool, step, UNITS, WAYS)

        @block.scalar
        def _(act):
            def take(u, c):
                act.wait_ge(summed, NSTEP * u + (4 if c == 0 else NSTEP))
                at_least(act, o_stored[c], 16 * u)
                nc.scalar.copy(o[c][:], total[:]).then_inc(o_taken, 1)

            def step(u, way):
                for s in range(NSTEP):
                    if s == LAG and not is_first(u):
                        take(u - 1, 1)
                    if s == 4 + LAG:
                        take(u, 0)
                    for pair in range(2):
                        n = 2 * (NSTEP * u + s) + pair
                        act.wait_ge(key_ready, n + 1)
                        if pair == 0:
                            at_least(act, summed, NSTEP * u + s - E_RING + 1)
                        nc.scalar.activation(e[s % E_RING][:, 2 * pair:2 * pair + 2, offset(s):GN],
                                             by_key[pair][:, :, offset(s):GN], ACT.Exp, scale=QUERY_SCALE).then_inc(weights_ready, 1)
            pipelined(act, step, UNITS, WAYS)
            take(UNITS - 1, 1)

        @block.vector
        def _(dve):
            def piece(u, way, m):
                h, n = m // NP_HEAD, m % NP_HEAD
                i, lo = PIECES[n]
                bank = by_query[m % 3]
                width = min((i + 1) * P - lo, GN)
                waits_apart(dve, (query_ready, NP_UNIT * u + m + 1))
                if lo + GN <= i * P:
                    ins = nc.vector.tensor_reduce(tops0[:, h, i - 4:i - 3], bank[:], AX_X, ALU.max)
                else:
                    ins = nc.vector.tensor_tensor_reduce(unused[m % 3][:, 0:width], bank[:, 0:width], mask[:, GN - width:GN],
                                                         1.0, 3 * LOW, ALU.add, ALU.max, tops[:, h, i:i + 1])
                ins.then_inc(query_read, 1)

            def split_maxima(u):
                at = SPLITS * u
                dve.wait_ge(query_read, NP_UNIT * (u + 1))
                nc.vector.tensor_tensor(tops[:, :, 4:8], tops[:, :, 4:8], tops0[:], ALU.max).then_inc(split, 1)
                dve.wait_ge(split, at + 1)
                at_least(dve, rows_turned, u)
                nc.vector.tensor_scalar(minus[:, 0], tops[:], -1.0, None, ALU.mult).then_inc(split, 1)
                dve.wait_ge(split, at + 2)
                nc.vector.scalar_tensor_tensor(rest[:], tops[:], -1.0, minus[:, 0], ALU.mult, ALU.subtract).then_inc(split, 1)
                dve.wait_ge(split, at + 3)
                nc.vector.tensor_copy(minus[:, 1], rest[:]).then_inc(split, 1)
                dve.wait_ge(split, at + 4)
                nc.vector.tensor_tensor(minus[:, 2], rest[:], minus[:, 1], ALU.subtract).then_inc(split, 1)

            def take_rows(u, way):
                dve.wait_ge(rows_turned, u + 1)
                at_least(dve, rows_placed, 48 * u)
                nc.vector.tensor_copy(rows[:], by_query[TURN_AT % 3][:].bitcast(BF16)[0:PARTS * HG * QBLOCKS, 0:P]).then_inc(rows_taken, 1)

            def step(u, way):
                for m in range(NP_UNIT):
                    if m == TURN_AT and not is_first(u):
                        take_rows(u - 1, (way - 1) % WAYS)
                    piece(u, way, m)
                split_maxima(u)
            dve.wait_ge(consts, 5)
            pipelined(dve, step, UNITS, WAYS)
            take_rows(UNITS - 1, WAYS - 1)

        @block.tensor
        def _(pe):
            def piece(u, way, m):
                h, (i, lo) = m // NP_HEAD, PIECES[m % NP_HEAD]
                if m == 0:
                    pe.wait_ge(loaded[way], LOADS * (u - way) * (16 // WAYS) + 16 * LOADS)
                if m == TURN_AT and not is_first(u):
                    at_least(pe, rows_taken, u)
                else:
                    at_least(pe, query_read, NP_UNIT * u + m - 2)
                width = min((i + 1) * P - lo, GN)
                nc.tensor.matmul(by_query[m % 3][:, 0:width], q[way][0:ROWS, h, i * P:(i + 1) * P],
                                 k[way][0:ROWS, h, lo:lo + width], start=True, stop=True).then_inc(query_ready, 1)

            def turn_rows(u, way):
                pe.wait_ge(split, SPLITS * (u + 1))
                if not is_last(u, UNITS):
                    pe.wait_ge(query_read, NP_UNIT * (u + 1) + TURN_AT - 2)
                nc.tensor.transpose(by_query[TURN_AT % 3][:].bitcast(BF16)[0:PARTS * HG * QBLOCKS, 0:P],
                                    minus[:].rearrange("p a h i -> p (a h i)"), identity16[:]).then_inc(rows_turned, 1)

            def scores(u, way, s, pair):
                c, j = STEPS[s]
                n = 2 * (NSTEP * u + s) + pair
                if s == 0 and pair == 0:
                    pe.wait_ge(rows_placed, 48 * (u + 1))
                at_least(pe, weights_ready, n - 1)
                for h in (2 * pair, 2 * pair + 1):
                    ins = nc.tensor.matmul(by_key[pair][:, h % 2, offset(s):GN], k[way][0:ROWS + PARTS, h, j * P:(j + 1) * P],
                                           q[way][0:ROWS + PARTS, h, c * GN + offset(s):(c + 1) * GN], start=True, stop=True)
                ins.then_inc(key_ready, 1)

            def weigh(u, way, s):
                c, j = STEPS[s]
                if j == 0:
                    if c == 0:
                        pe.wait_ge(v_loaded[way], (u - way) * (16 // WAYS) + 16)
                    at_least(pe, o_taken, 2 * u + c)
                if diagonal(s):
                    pe.wait_ge(masked, DIAGONAL * u + diagonals_to(s))
                else:
                    pe.wait_ge(weights_ready, 2 * (NSTEP * u + s + 1))
                for h in range(HG):
                    ins = nc.tensor.matmul(total[VW * h:VW * (h + 1), offset(s):GN], v[way][:, j, VW * h:VW * (h + 1)],
                                           e[s % E_RING][:, h, offset(s):GN], start=(j == 0), stop=(j == 4 * c + 3))
                ins.then_inc(summed, 1)

            def ahead(u, way, m):
                if m == TURN_AT and not is_first(u):
                    turn_rows(u - 1, (way - 1) % WAYS)
                if not (isinstance(u, int) and u >= UNITS):
                    piece(u, way, m)

            pe.wait_ge(consts, 9)
            for m in range(NP_UNIT):
                ahead(0, 0, m)
            for m in range(AHEAD):
                ahead(1, 1, m)

            def step(u, way):
                order = [(u + 1, (way + 1) % WAYS, m) for m in range(AHEAD, NP_UNIT)] + [(u + 2, (way + 2) % WAYS, m) for m in range(AHEAD)]
                if is_last(u, UNITS):
                    order = []
                def pieces(n):
                    for at in order[SHARE[n]:SHARE[n + 1]]:
                        ahead(*at)
                for s in range(NSTEP):
                    scores(u, way, s, 0)
                    pieces(3 * s)
                    scores(u, way, s, 1)
                    pieces(3 * s + 1)
                    if s >= LAG:
                        weigh(u, way, s - LAG)
                    elif not is_first(u):
                        weigh(u - 1, (way - 1) % WAYS, NSTEP - LAG + s)
                    pieces(3 * s + 2)
            pipelined(pe, step, UNITS, WAYS)
            for s in range(NSTEP - LAG, NSTEP):
                weigh(UNITS - 1, WAYS - 1, s)


def attention_out(nc, x_in, o_in, w_o, x_out):
    with ExitStack() as ctx:
        sb = lambda n, s, d: ctx.enter_context(nc.sbuf_tensor(f"out_{n}", s, d))
        ps = lambda n, s, d=F32: ctx.enter_context(nc.psum_tensor(f"out_{n}", s, d))
        sem = lambda n: ctx.enter_context(nc.semaphore(f"out_{n}"))
        UG = HEADS // HG
        w_f = sb("w_f", [P, KC * D], F32)
        w_high = sb("w_high", [P, KC * D], F32R)
        w_low = sb("w_low", [P, KC * D], F32R)
        identity = sb("identity", [P, P], F32)
        o = [sb(f"o{i}", [P, UG, GN], F32) for i in range(2)]
        x = [sb(f"x{i}", [P, GT, D], F32) for i in range(2)]
        y = [sb(f"y{i}", [P, GT, D], F32) for i in range(2)]
        inverse = sb("inverse", [P, GT, HEADS], F32)
        merged = sb("merged", [P, GT, D], F32)
        high = sb("high", [P, KC, GN], F32R)
        low = sb("low", [P, KC, GN], F32R)
        sums = [ps(f"sums{i}", [P, UG * P]) for i in range(2)]
        turned = ps("turned", [P, KC, GN])
        out = ps("out", [P, GT, D])
        consts, w_loaded, w_ready = sem("consts"), sem("w_loaded"), sem("w_ready")
        loaded, x_loaded = [sem("loaded0"), sem("loaded1")], [sem("x_loaded0"), sem("x_loaded1")]
        sums_ready, inverse_ready, merged_ready = sem("sums_ready"), sem("inverse_ready"), sem("merged_ready")
        turned_ready, high_ready, low_ready, out_ready, y_ready = (sem(n) for n in ("turned_ready", "high_ready", "low_ready", "out_ready", "y_ready"))
        stored = [sem("stored0"), sem("stored1")]
        block = ctx.enter_context(nc.Block())

        @block.sync
        def _(sp):
            sp.dma_start(w_f[:].rearrange("p (c n) -> p c n", c=KC), w_o.rearrange("(c p) n -> p c n", p=P)).then_inc(w_loaded, 16)

            def load(g, slot, b):
                at_least(sp, y_ready, g - 1)
                src = o_in[bass.ds(b * UG, UG), :, slot * GN:(slot + 1) * GN]
                sp.dma_start(o[slot][:], src.rearrange("u p n -> p u n")).then_inc(loaded[slot], 16)
                sp.dma_start(x[slot][:], group_rows(x_in, g)).then_inc(x_loaded[slot], 16)

            def store(g, slot):
                sp.wait_ge(y_ready, g + 1)
                sp.dma_start(group_rows(x_out, g), y[slot][:]).then_inc(stored[slot], 16)
            load(0, 0, 0)
            load(1, 1, 0)
            with sp.Fori(0, BATCH - 1) as b:
                for slot in range(2):
                    store(2 * b + slot, slot)
                    load(2 * b + 2 + slot, slot, b + 1)
            for slot in range(2):
                store(GROUPS - 2 + slot, slot)
            for s in stored:
                sp.wait_ge(s, 8 * GROUPS)

        @block.gpsimd
        def _(pool):
            fill_identity(nc, identity, consts)

        @block.scalar
        def _(act):
            def step(g, slot):
                act.wait_ge(turned_ready, g + 1)
                at_least(act, out_ready, g)
                nc.scalar.copy(high[:], turned[:]).then_inc(high_ready, 1)
            pipelined(act, step, GROUPS)

        @block.vector
        def _(dve):
            dve.wait_ge(w_loaded, 16)
            nc.vector.tensor_copy(w_high[:], w_f[:]).then_inc(w_ready, 1)
            dve.wait_ge(w_ready, 1)
            nc.vector.tensor_tensor(w_low[:], w_f[:], w_high[:].bitcast(F32), ALU.subtract).then_inc(w_ready, 1)

            def finish(g, slot):
                dve.wait_ge(out_ready, g + 1)
                dve.wait_ge(x_loaded[slot], 8 * g + 16 - 8 * slot)
                at_least(dve, stored[slot], 8 * g - 8 * slot)
                nc.vector.tensor_tensor(y[slot][:], out[:], x[slot][:], ALU.add).then_inc(y_ready, 1)

            def step(g, slot):
                at_least(dve, turned_ready, g)
                for t in range(GT):
                    n = GT * g + t
                    s = sums[t % 2][:].rearrange("p (h n) -> p h n", n=VW)
                    dve.wait_ge(sums_ready, n + 1)
                    nc.vector.reciprocal(inverse[:, t, :], s[:, :, HD]).then_inc(inverse_ready, 1)
                    dve.wait_ge(inverse_ready, n + 1)
                    nc.vector.tensor_tensor(merged[:, t, :].rearrange("p (h n) -> p h n", n=HD), s[:, :, 0:HD],
                                            inverse[:, t, :].unsqueeze(2).broadcast_to([P, HEADS, HD]), ALU.mult).then_inc(merged_ready, 1)
                if not is_first(g):
                    finish(g - 1, 1 - slot)
                dve.wait_ge(high_ready, g + 1)
                nc.vector.tensor_tensor(low[:], turned[:], high[:].bitcast(F32), ALU.subtract).then_inc(low_ready, 1)
            pipelined(dve, step, GROUPS)
            finish(GROUPS - 1, 1)

        @block.tensor
        def _(pe):
            pe.wait_ge(consts, 2)
            pe.wait_ge(w_ready, 2)

            def step(g, slot):
                pe.wait_ge(loaded[slot], 8 * g + 16 - 8 * slot)
                for t in range(GT):
                    n = GT * g + t
                    at_least(pe, merged_ready, n - 1)
                    for u in range(UG):
                        ins = nc.tensor.transpose(sums[t % 2][:, u * P:(u + 1) * P], o[slot][:, u, t * P:(t + 1) * P], identity[:])
                    ins.then_inc(sums_ready, 1)
                at_least(pe, low_ready, g)
                pe.wait_ge(merged_ready, GT * (g + 1))
                for c in range(KC):
                    for t in range(GT):
                        ins = nc.tensor.transpose(turned[:, c, t * P:(t + 1) * P], merged[:, t, c * P:(c + 1) * P], identity[:])
                ins.then_inc(turned_ready, 1)
                pe.wait_ge(low_ready, g + 1)
                at_least(pe, y_ready, g)
                for t in range(GT):
                    ts = slice(t * P, (t + 1) * P)
                    ins = product(nc, out[:, t, :], [(high[:, c, ts], low[:, c, ts], w_high[:, c * D:(c + 1) * D], w_low[:, c * D:(c + 1) * D])
                                                     for c in range(KC)])
                ins.then_inc(out_ready, 1)
            pipelined(pe, step, GROUPS)
HIDDEN = 768
HC = HIDDEN // P
DEQUANT = float(np.float32(1.0 / 127.0))


def swiglu_ffn(nc, x_in, gate_up, down, x_out):
    with ExitStack() as ctx:
        sb = lambda n, s, d: ctx.enter_context(nc.sbuf_tensor(f"ffn_{n}", s, d))
        ps = lambda n, s: ctx.enter_context(nc.psum_tensor(f"ffn_{n}", s, F32))
        sem = lambda n: ctx.enter_context(nc.semaphore(f"ffn_{n}"))
        W1 = KC * 2 * HIDDEN
        W2 = HC * D
        w_int = sb("w_int", [P, W1 + W2], I32)
        w_f = sb("w_f", [P, W1 + W2], F32)
        w_high = sb("w_high", [P, W1 + W2], F32R)
        w_low = sb("w_low", [P, W1 + W2], F32R)
        identity = sb("identity", [P, P], F32)
        gated = [sb(f"gated{i}", [P, GN], F32) for i in range(2)]
        hidden = [sb(f"hidden{i}", [P, GN], F32) for i in range(2)]
        h_high = sb("h_high", [P, HC, GN], F32R)
        h_low = sb("h_low", [P, HC, GN], F32R)
        y = [sb(f"y{i}", [P, GT, D], F32) for i in range(2)]
        turned = ps("turned", [P, KC, GN])
        gate = [ps(f"gate{i}", [P, GN]) for i in range(2)]
        up = [ps(f"up{i}", [P, GN]) for i in range(2)]
        out = ps("out", [P, GT, D])
        f = Front(nc, ctx, "ffn", turned)
        w_loaded, w_ready, identity_ready = sem("w_loaded"), sem("w_ready"), sem("identity_ready")
        gate_ready, up_ready = sem("gate_ready"), sem("up_ready")
        gated_ready = sem("gated_ready")
        hidden_ready = sem("hidden_ready")
        h_high_ready, h_low_ready = sem("h_high_ready"), sem("h_low_ready")
        down_done = sem("down_done")
        y_ready = sem("y_ready")
        y_stored = [sem("y_stored_even"), sem("y_stored_odd")]

        def w1(column, c):
            s = slice(c * 2 * HIDDEN + column, c * 2 * HIDDEN + column + P)
            return w_high[:, s], w_low[:, s]

        def w2(c):
            s = slice(W1 + c * D, W1 + (c + 1) * D)
            return w_high[:, s], w_low[:, s]

        block = ctx.enter_context(nc.Block())

        @block.sync
        def _(sp):
            sp.dma_start(w_int[:, 0:W1].rearrange("p (c n) -> p c n", c=KC),
                         gate_up.rearrange("(c p) n -> p c n", p=P)).then_inc(w_loaded, 16)
            sp.dma_start(w_int[:, W1:W1 + W2].rearrange("p (c n) -> p c n", c=HC),
                         down.rearrange("(c p) n -> p c n", p=P)).then_inc(w_loaded, 16)
            f.load(x_in, 0, 0)
            f.load(x_in, 1, 1)

            def store(g, slot):
                sp.wait_ge(y_ready, g + 1)
                sp.dma_start(group_rows(x_out, g), y[slot][:]).then_inc(y_stored[slot], 16)

            def step(g, slot):
                if not (isinstance(g, int) and g + 2 >= GROUPS):
                    f.load(x_in, g + 2, slot)
                if not is_first(g):
                    store(g - 1, 1 - slot)
            pipelined(sp, step, GROUPS)
            store(GROUPS - 1, 1)
            for s in y_stored:
                sp.wait_ge(s, 8 * GROUPS)

        @block.gpsimd
        def _(pool):
            fill_identity(nc, identity, identity_ready)

            def step(g, slot):
                for c in range(HC):
                    n = g * HC + c
                    waits_apart(pool, (hidden_ready, n + 1), (down_done, n + 1 - HC))
                    nc.gpsimd.tensor_copy(h_high[:, c, :], hidden[c % 2][:]).then_inc(h_high_ready, 1)
                    pool.wait_ge(h_high_ready, n + 1)
                    nc.gpsimd.tensor_tensor(h_low[:, c, :], hidden[c % 2][:], h_high[:, c, :].bitcast(F32),
                                            ALU.subtract).then_inc(h_low_ready, 1)
            pipelined(pool, step, GROUPS)

        @block.scalar
        def _(act):
            f.take_high(0, 0)

            def step(g, slot):
                for c in range(HC):
                    n = g * HC + c
                    act.wait_ge(gate_ready, n + 1)
                    at_least(act, hidden_ready, n - 1)
                    nc.scalar.activation(gated[c % 2][:], gate[c % 2][:], ACT.Silu).then_inc(gated_ready, 1)
                    if c == 3 and not is_last(g, GROUPS):
                        at_least(act, up_ready, HC * g)
                        f.take_high(g + 1, 1 - slot)
            pipelined(act, step, GROUPS)

        @block.vector
        def _(dve):
            dve.wait_ge(w_loaded, 32)
            nc.vector.tensor_scalar(w_f[:], w_int[:], DEQUANT, None, ALU.mult).then_inc(w_ready, 1)
            dve.wait_ge(w_ready, 1)
            nc.vector.tensor_copy(w_high[:], w_f[:]).then_inc(w_ready, 1)
            dve.wait_ge(w_ready, 2)
            nc.vector.tensor_tensor(w_low[:], w_f[:], w_high[:].bitcast(F32), ALU.subtract).then_inc(w_ready, 1)
            f.normalise(0, 0)
            f.take_low(0, 0)

            def finish(g, slot):
                dve.wait_ge(down_done, HC * (g + 1))
                at_least(dve, y_stored[slot], 8 * g - 8 * slot)
                nc.vector.tensor_tensor(y[slot][:], out[:], f.resid[slot][:], ALU.add).then_inc(y_ready, 1)

            def step(g, slot):
                for c in range(HC):
                    n = g * HC + c
                    dve.wait_ge(gated_ready, n + 1)
                    dve.wait_ge(up_ready, n + 1)
                    at_least(dve, h_low_ready, n - 1)
                    nc.vector.tensor_tensor(hidden[c % 2][:], gated[c % 2][:], up[c % 2][:], ALU.mult).then_inc(hidden_ready, 1)
                    if c == 1 and not is_first(g):
                        finish(g - 1, 1 - slot)
                    if c == 1 and not is_last(g, GROUPS):
                        f.normalise(g + 1, 1 - slot, [(y_ready, g)])
                    if c == 4 and not is_last(g, GROUPS):
                        f.take_low(g + 1, 1 - slot)
            pipelined(dve, step, GROUPS)
            finish(GROUPS - 1, 1)

        @block.tensor
        def _(pe):
            pe.wait_ge(identity_ready, 2)
            f.turn(0, identity[:])
            pe.wait_ge(w_ready, 3)

            def down_chunk(n, c):
                pe.wait_ge(h_low_ready, n + 1)
                for t in range(GT):
                    ts = slice(t * P, (t + 1) * P)
                    ins = product(nc, out[:, t, :], [(h_high[:, c, ts], h_low[:, c, ts], *w2(c))],
                                  start=(c == 0 and t % 2 == 0), stop=(c == HC - 1), shared=True)
                ins.then_inc(down_done, 1)

            def step(g, slot):
                pe.wait_ge(f.low_ready, g + 1)
                for c in range(HC):
                    n = g * HC + c
                    at_least(pe, hidden_ready, n - 1)
                    for bank, base, ready in ((gate, 0, gate_ready), (up, HIDDEN, up_ready)):
                        product(nc, bank[c % 2][:], [(*w1(base + c * P, k), f.high[slot][:, k, :], f.low[slot][:, k, :])
                                                     for k in range(KC)]).then_inc(ready, 1)
                    if c >= 2:
                        if c == 2:
                            at_least(pe, y_ready, g)
                        down_chunk(n - 2, c - 2)
                    elif not is_first(g):
                        down_chunk(n - 2, HC - 2 + c)
                    if c == 3 and not is_last(g, GROUPS):
                        f.turn(g + 1, identity[:])
            pipelined(pe, step, GROUPS)
            down_chunk(GROUPS * HC - 2, HC - 2)
            down_chunk(GROUPS * HC - 1, HC - 1)
SCORE_SCALE = float(D) ** -0.5


def column_attention(nc, x_in, w_qkv, x_out):
    with ExitStack() as ctx:
        sb = lambda n, s, d: ctx.enter_context(nc.sbuf_tensor(f"col_{n}", s, d))
        ps = lambda n, s, d=F32: ctx.enter_context(nc.psum_tensor(f"col_{n}", s, d))
        sem = lambda n: ctx.enter_context(nc.semaphore(f"col_{n}"))
        W = KC * 3 * D
        NB = SEQ // P
        BLOCKS = BATCH * NB
        FILLS = 12
        w_f = sb("w_f", [P, W], F32)
        w_high = sb("w_high", [P, W], F32R)
        w_low = sb("w_low", [P, W], F32R)
        identity = sb("identity", [P, P], F32)
        qk_high = sb("qk_high", [P, 2 * KC, SEQ], F32R)
        qk_low = sb("qk_low", [P, 2 * KC, SEQ], F32R)
        v_high = sb("v_high", [P, NB, D], F32R)
        v_low = sb("v_low", [P, NB, D], F32R)
        weights = [sb(f"weights{i}", [P, SEQ], F32) for i in range(2)]
        t_high = [sb(f"t_high{i}", [P, NB, P], F32R) for i in range(2)]
        t_low = [sb(f"t_low{i}", [P, NB, P], F32R) for i in range(2)]
        top = sb("top", [P, 4], F32)
        bias = sb("bias", [P, 4], F32)
        total = sb("total", [P, 4], F32)
        inverse = sb("inverse", [P, 4], F32)
        x = [sb(f"xb{i}", [P, D], F32) for i in range(2)]
        y = [sb(f"y{i}", [P, D], F32) for i in range(2)]
        turned = ps("turned", [P, KC, GN])
        scores = [ps(f"scores{i}", [P, SEQ]) for i in range(2)]
        out = [ps(f"out{i}", [P, GN]) for i in range(2)]
        f = Front(nc, ctx, "col", turned)
        consts, w_loaded, w_ready = sem("consts"), sem("w_loaded"), sem("w_ready")
        fill_ready, fill_high, fill_low = sem("fill_ready"), sem("fill_high"), sem("fill_low")
        scores_ready = sem("scores_ready")
        top_ready, bias_ready = sem("top_ready"), sem("bias_ready")
        weights_ready = sem("weights_ready")
        t_turned, t_high_ready, t_low_ready = sem("t_turned"), sem("t_high_ready"), sem("t_low_ready")
        out_ready = sem("out_ready")
        inverse_ready, y_ready = sem("inverse_ready"), sem("y_ready")
        xb_loaded = [sem("xb_loaded0"), sem("xb_loaded1")]
        stored = [sem("stored0"), sem("stored1")]
        block = ctx.enter_context(nc.Block())

        def bank(i):
            return scores[i // 2][:, (i % 2) * GN:(i % 2 + 1) * GN]

        def fill_target(i, lo):
            if i < 8:
                a = qk_low if lo else qk_high
                return a[:, i % 4, (i // 4) * GN:(i // 4 + 1) * GN]
            a = v_low if lo else v_high
            return a[:, 2 * (i - 8):2 * (i - 8) + 2, :].rearrange("p t n -> p (t n)")

        def rows(ap, n):
            return ap[bass.ds(n * P, P), :]

        def batches(engine, step):
            step(0)
            with engine.Fori(1, BATCH - 1) as b:
                step(b)
            step(BATCH - 1)

        FRONT_AT = {3: 0, 6: 1}

        @block.sync
        def _(sp):
            sp.dma_start(w_f[:].rearrange("p (c n) -> p c n", c=KC), w_qkv.rearrange("(c p) n -> p c n", p=P)).then_inc(w_loaded, 16)
            f.load(x_in, 0, 0)
            f.load(x_in, 1, 1)

            def store(n, slot):
                sp.wait_ge(y_ready, n + 1)
                sp.dma_start(rows(x_out, n), y[slot][:]).then_inc(stored[slot], 16)

            def step(b):
                if not is_last(b, BATCH):
                    f.load(x_in, 2 * b + 2, 0)
                    f.load(x_in, 2 * b + 3, 1)
                for j in range(NB):
                    n = NB * b + j
                    if j >= 2 or not is_first(b):
                        store(n - 2, j % 2)
                    sp.dma_start(x[j % 2][:], rows(x_in, n)).then_inc(xb_loaded[j % 2], 16)
            batches(sp, step)
            store(BLOCKS - 2, 0)
            store(BLOCKS - 1, 1)
            for s in stored:
                sp.wait_ge(s, 8 * BLOCKS)

        @block.gpsimd
        def _(pool):
            fill_identity(nc, identity, consts)

        @block.scalar
        def _(act):
            f.take_high(0, 0)
            f.take_high(1, 1)

            def high(n, slot):
                act.wait_ge(t_turned, n + 1)
                at_least(act, out_ready, n - 1)
                nc.scalar.copy(t_high[slot][:], turned[:].rearrange("p c (t n) -> p (c t) n", n=P)).then_inc(t_high_ready, 1)

            def step(b):
                for i in range(FILLS):
                    if i == 4 and not is_first(b):
                        high(NB * b - 1, 1)
                    act.wait_ge(fill_ready, FILLS * b + i + 1)
                    nc.scalar.copy(fill_target(i, False), bank(i % 4)).then_inc(fill_high, 1)
                for j in range(NB):
                    n = NB * b + j
                    act.wait_ge(bias_ready, n + 1)
                    at_least(act, t_turned, n - 1)
                    nc.scalar.activation(weights[j % 2][:], scores[j % 2][:], ACT.Exp, bias=bias[:, j % 4:j % 4 + 1],
                                         scale=SCORE_SCALE, accum_out=total[:, j % 4:j % 4 + 1]).then_inc(weights_ready, 1)
                    if j >= 1:
                        high(n - 1, (j - 1) % 2)
                    if j in FRONT_AT and not is_last(b, BATCH):
                        f.take_high(2 * b + 2 + FRONT_AT[j], FRONT_AT[j])
            batches(act, step)
            high(BLOCKS - 1, 1)

        @block.vector
        def _(dve):
            dve.wait_ge(w_loaded, 16)
            nc.vector.tensor_copy(w_high[:], w_f[:]).then_inc(w_ready, 1)
            dve.wait_ge(w_ready, 1)
            nc.vector.tensor_tensor(w_low[:], w_f[:], w_high[:].bitcast(F32), ALU.subtract).then_inc(w_ready, 1)
            for g in range(2):
                f.normalise(g, g, keep=False)
                f.take_low(g, g)

            def low(n, slot):
                dve.wait_ge(t_high_ready, n + 1)
                nc.vector.tensor_tensor(t_low[slot][:], turned[:].rearrange("p c (t n) -> p (c t) n", n=P),
                                        t_high[slot][:].bitcast(F32), ALU.subtract).then_inc(t_low_ready, 1)

            def finish(n, j):
                dve.wait_ge(out_ready, n + 1)
                nc.vector.reciprocal(inverse[:, j % 4:j % 4 + 1], total[:, j % 4:j % 4 + 1]).then_inc(inverse_ready, 1)
                dve.wait_ge(xb_loaded[j % 2], 8 * (n - j % 2) + 16)
                at_least(dve, stored[j % 2], 8 * (n - j % 2))
                dve.wait_ge(inverse_ready, n + 1)
                nc.vector.scalar_tensor_tensor(y[j % 2][:], out[j % 2][:, 0:D], inverse[:, j % 4:j % 4 + 1], x[j % 2][:],
                                               ALU.mult, ALU.add).then_inc(y_ready, 1)

            def step(b):
                for i in range(FILLS):
                    if not is_first(b):
                        if i == 4:
                            low(NB * b - 1, 1)
                            finish(NB * b - 2, NB - 2)
                        if i == 8:
                            finish(NB * b - 1, NB - 1)
                    dve.wait_ge(fill_high, FILLS * b + i + 1)
                    nc.vector.tensor_tensor(fill_target(i, True), bank(i % 4), fill_target(i, False).bitcast(F32),
                                            ALU.subtract).then_inc(fill_low, 1)
                for j in range(NB):
                    n = NB * b + j
                    dve.wait_ge(scores_ready, n + 1)
                    nc.vector.reduce_max(top[:, j % 4:j % 4 + 1], scores[j % 2][:], AX_X).then_inc(top_ready, 1)
                    dve.wait_ge(top_ready, n + 1)
                    nc.vector.tensor_scalar(bias[:, j % 4:j % 4 + 1], top[:, j % 4:j % 4 + 1], -SCORE_SCALE, None, ALU.mult).then_inc(bias_ready, 1)
                    if j >= 1:
                        low(n - 1, (j - 1) % 2)
                    if j >= 2:
                        finish(n - 2, j - 2)
                    if not is_last(b, BATCH):
                        if j in FRONT_AT:
                            f.take_low(2 * b + 2 + FRONT_AT[j], FRONT_AT[j])
                        if j + 2 in FRONT_AT:
                            f.normalise(2 * b + 2 + FRONT_AT[j + 2], FRONT_AT[j + 2], keep=False)
            batches(dve, step)
            low(BLOCKS - 1, 1)
            finish(BLOCKS - 2, NB - 2)
            finish(BLOCKS - 1, NB - 1)

        @block.tensor
        def _(pe):
            pe.wait_ge(consts, 2)
            f.turn(0, identity[:])
            f.turn(1, identity[:])
            pe.wait_ge(w_ready, 2)

            def w(c, column, width):
                s = slice(c * 3 * D + column, c * 3 * D + column + width)
                return w_high[:, s], w_low[:, s]

            def fill(b, i):
                if i == 0:
                    pe.wait_ge(f.low_ready, 2 * b + 1)
                if i == 4:
                    pe.wait_ge(f.low_ready, 2 * b + 2)
                if i < 4:
                    at_least(pe, weights_ready, NB * b)
                    at_least(pe, fill_low, FILLS * b)
                else:
                    pe.wait_ge(fill_low, FILLS * b + i - 3)
                if i < 8:
                    slot = i // 4
                    ins = product(nc, bank(i % 4), [(*w(c, (i % 4) * P, P), f.high[slot][:, c, :], f.low[slot][:, c, :]) for c in range(KC)])
                else:
                    for half in range(2):
                        t = 2 * (i - 8) + half
                        slot, ts = t // GT, slice((t % GT) * P, (t % GT + 1) * P)
                        ins = product(nc, bank(i % 4)[:, half * D:(half + 1) * D],
                                      [(f.high[slot][:, c, ts], f.low[slot][:, c, ts], *w(c, 2 * D, D)) for c in range(KC)])
                ins.then_inc(fill_ready, 1)

            def turn(n, slot):
                pe.wait_ge(weights_ready, n + 1)
                at_least(pe, t_low_ready, n)
                for c in range(NB):
                    ins = nc.tensor.transpose(turned[:, c // GT, (c % GT) * P:(c % GT + 1) * P], weights[slot][:, c * P:(c + 1) * P], identity[:])
                ins.then_inc(t_turned, 1)

            def weigh(n, slot):
                pe.wait_ge(t_low_ready, n + 1)
                at_least(pe, y_ready, n - 1)
                product(nc, out[slot][:, 0:D], [(t_high[slot][:, c, :], t_low[slot][:, c, :], v_high[:, c, :], v_low[:, c, :])
                                                for c in range(NB)]).then_inc(out_ready, 1)

            def step(b):
                for i in range(FILLS):
                    if not is_first(b):
                        if i == 4:
                            turn(NB * b - 1, 1)
                            weigh(NB * b - 2, 0)
                        if i == 8:
                            weigh(NB * b - 1, 1)
                    fill(b, i)
                pe.wait_ge(fill_low, FILLS * (b + 1))
                for j in range(NB):
                    n = NB * b + j
                    if j >= 2:
                        pe.wait_ge(weights_ready, n - 1)
                    for half in range(2):
                        hs, js = slice(half * GN, (half + 1) * GN), slice(j * P, (j + 1) * P)
                        ins = product(nc, scores[j % 2][:, hs], [(qk_high[:, KC + c, js], qk_low[:, KC + c, js], qk_high[:, c, hs], qk_low[:, c, hs])
                                                                 for c in range(KC)])
                    ins.then_inc(scores_ready, 1)
                    if j >= 1:
                        if j - 1 in FRONT_AT and not is_last(b, BATCH):
                            pe.wait_ge(f.low_ready, 2 * b + 3 + FRONT_AT[j - 1])
                        turn(n - 1, (j - 1) % 2)
                    if j >= 2:
                        weigh(n - 2, j % 2)
                    if j in FRONT_AT and not is_last(b, BATCH):
                        pe.wait_ge(t_low_ready, n)
                        f.turn(2 * b + 2 + FRONT_AT[j], identity[:])
            batches(pe, step)
            turn(BLOCKS - 1, 1)
            weigh(BLOCKS - 2, 0)
            weigh(BLOCKS - 1, 1)
EXPERTS = 16
TOPK = 2
CHUNKS = EXPERTS + 2


class Router:

    STEPS = 8 + 2 * GT + 5

    def __init__(self, nc, ctx, logits):
        sb = lambda n, s, d=F32: ctx.enter_context(nc.sbuf_tensor(f"router_{n}", s, d))
        sem = lambda n: ctx.enter_context(nc.semaphore(f"router_{n}"))
        self.nc, self.logits = nc, logits
        self.centred, self.e, self.p, self.hit, self.hit1 = (sb(n, [P, GT, EXPERTS]) for n in ("centred", "e", "p", "hit", "hit1"))
        self.cw = [sb(f"cw{i}", [P, GT, EXPERTS]) for i in range(2)]
        self.top, self.total, self.inverse = (sb(n, [P, GT]) for n in ("top", "total", "inverse"))
        self.best = sb("best", [P, GT, 8])
        self.where, self.where_f = sb("where", [P, GT, 8], U32), sb("where_f", [P, GT, 8])
        self.number = sb("number", [P, EXPERTS])
        self.logits_ready, self.chain, self.e_ready = sem("logits_ready"), sem("chain"), sem("e_ready")

    def choose(self, g, slot):
        dve = self.nc.vector
        base, n = self.STEPS * g, [0]

        def chained(ins):
            n[0] += 1
            ins.then_inc(self.chain, 1)
            return n[0]

        def wait():
            waits_apart(dve, (self.chain, base + n[0]))
        wide = [P, GT, EXPERTS]
        over = lambda a: a.unsqueeze(2).broadcast_to(wide)
        l = self.logits.rearrange("p (t e) -> p t e", e=EXPERTS)
        dve.wait_ge(self.logits_ready, g + 1)
        chained(dve.reduce_max(self.top[:], l, AX_X)); wait()
        chained(dve.tensor_tensor(self.centred[:], l, over(self.top[:]), ALU.subtract))
        dve.wait_ge(self.e_ready, g + 1)
        chained(dve.reduce_sum(self.total[:], self.e[:], AX_X)); wait()
        chained(dve.reciprocal(self.inverse[:], self.total[:])); wait()
        chained(dve.tensor_tensor(self.p[:], self.e[:], over(self.inverse[:]), ALU.mult)); wait()
        for t in range(GT):
            chained(dve.max(self.best[:, t, :], self.p[:, t, :]))
        wait()
        for t in range(GT):
            chained(dve.max_index(self.where[:, t, :], self.best[:, t, :], self.p[:, t, :]))
        wait()
        chained(dve.tensor_copy(self.where_f[:], self.where[:])); wait()
        number = self.number[:].unsqueeze(1).broadcast_to(wide)
        chained(dve.tensor_tensor(self.hit[:], number, over(self.where_f[:, :, 0]), ALU.is_equal))
        chained(dve.tensor_tensor(self.hit1[:], number, over(self.where_f[:, :, 1]), ALU.is_equal)); wait()
        chained(dve.tensor_tensor(self.hit[:], self.hit[:], over(self.best[:, :, 0]), ALU.mult))
        chained(dve.tensor_tensor(self.hit1[:], self.hit1[:], over(self.best[:, :, 1]), ALU.mult)); wait()
        chained(dve.tensor_tensor(self.cw[slot][:], self.hit[:], self.hit1[:], ALU.add)); wait()
        while n[0] < self.STEPS:
            dve.sem_inc(self.chain, 1)
            n[0] += 1

    def exponentials(self, g):
        act = self.nc.scalar
        act.wait_ge(self.chain, self.STEPS * g + 2)
        act.activation(self.e[:], self.centred[:], ACT.Exp).then_inc(self.e_ready, 1)


def experts(nc, x_in, w_router, gate_up, down, x_out):
    with ExitStack() as ctx:
        sb = lambda n, s, d: ctx.enter_context(nc.sbuf_tensor(f"moe_{n}", s, d))
        ps = lambda n, s: ctx.enter_context(nc.psum_tensor(f"moe_{n}", s, F32))
        sem = lambda n: ctx.enter_context(nc.semaphore(f"moe_{n}"))
        WC = KC * 2 * P + D
        W = CHUNKS * WC
        RING = 3
        HC = CHUNKS
        w_f = [sb(f"w_f{i}", [P, WC], F32) for i in range(2)]
        w_high = sb("w_high", [P, W], F32R)
        w_low = sb("w_low", [P, W], F32R)
        r_f = sb("r_f", [P, KC * EXPERTS], F32)
        r_high = sb("r_high", [P, KC * EXPERTS], F32R)
        r_low = sb("r_low", [P, KC * EXPERTS], F32R)
        identity = sb("identity", [P, P], F32)
        gated = [sb(f"gated{i}", [P, GN], F32) for i in range(2)]
        hidden = [sb(f"hidden{i}", [P, GN], F32) for i in range(2)]
        h_high = sb("h_high", [P, RING, GN], F32R)
        h_low = sb("h_low", [P, RING, GN], F32R)
        turned = ps("turned", [P, KC, GN])
        gate = [ps(f"gate{i}", [P, GN]) for i in range(2)]
        up = [ps(f"up{i}", [P, GN]) for i in range(2)]
        out = ps("out", [P, GT, D])
        f = Front(nc, ctx, "moe", turned)
        router = Router(nc, ctx, turned[:, 0, 0:GT * EXPERTS])
        w_loaded, w_split, w_ready, consts = [sem("w_loaded0"), sem("w_loaded1")], sem("w_split"), sem("w_ready"), sem("consts")
        r_loaded = sem("r_loaded")
        gate_ready, up_ready, gated_ready, hidden_ready = (sem(n) for n in ("gate_ready", "up_ready", "gated_ready", "hidden_ready"))
        h_high_ready, h_low_ready, down_done, out_read = (sem(n) for n in ("h_high_ready", "h_low_ready", "down_done", "out_read"))
        y_ready = sem("y_ready")
        y_stored = [sem("y_stored0"), sem("y_stored1")]

        def w1(c, kind, k):
            s = slice(c * WC + k * 2 * P + kind * P, c * WC + k * 2 * P + kind * P + P)
            return w_high[:, s], w_low[:, s]

        def w2(c):
            s = slice(c * WC + KC * 2 * P, (c + 1) * WC)
            return w_high[:, s], w_low[:, s]

        block = ctx.enter_context(nc.Block())

        @block.sync
        def _(sp):
            sp.dma_start(r_f[:].rearrange("p (c n) -> p c n", c=KC), w_router.rearrange("(c p) n -> p c n", p=P)).then_inc(r_loaded, 16)
            f.load(x_in, 0, 0)
            f.load(x_in, 1, 1)
            for c in range(CHUNKS):
                at_least(sp, w_split, 2 * c if c >= 2 else 0)
                sp.dma_start(w_f[c % 2][:, 0:KC * 2 * P].rearrange("p (c n) -> p c n", c=KC), gate_up[c].rearrange("(c p) n -> p c n", p=P)).then_inc(w_loaded[c % 2], 16)
                sp.dma_start(w_f[c % 2][:, KC * 2 * P:WC], down[c * P:(c + 1) * P, :]).then_inc(w_loaded[c % 2], 16)

            def store(g, slot):
                sp.wait_ge(y_ready, g + 1)
                sp.dma_start(group_rows(x_out, g), f.resid[slot][:]).then_inc(y_stored[slot], 16)

            def step(g, slot):
                if not (isinstance(g, int) and g + 2 >= GROUPS):
                    f.load(x_in, g + 2, slot)
                if not is_first(g):
                    store(g - 1, 1 - slot)
            pipelined(sp, step, GROUPS)
            store(GROUPS - 1, 1)
            for s in y_stored:
                sp.wait_ge(s, 8 * GROUPS)

        @block.gpsimd
        def _(pool):
            fill_identity(nc, identity, consts)
            nc.gpsimd.iota(router.number[:], [[1, EXPERTS]], base=0, channel_multiplier=0,
                           allow_small_or_imprecise_dtypes=True).then_inc(consts, 1)

            def step(g, slot):
                for c in range(HC):
                    n = g * HC + c
                    waits_apart(pool, (hidden_ready, n + 1), (down_done, n + 1 - RING))
                    nc.gpsimd.tensor_copy(h_high[:, c % RING, :], hidden[c % 2][:]).then_inc(h_high_ready, 1)
                    pool.wait_ge(h_high_ready, n + 1)
                    nc.gpsimd.tensor_tensor(h_low[:, c % RING, :], hidden[c % 2][:], h_high[:, c % RING, :].bitcast(F32),
                                            ALU.subtract).then_inc(h_low_ready, 1)
            pipelined(pool, step, GROUPS)

        @block.scalar
        def _(act):
            f.take_high(0, 0)

            def step(g, slot):
                router.exponentials(g)
                for c in range(HC):
                    n = g * HC + c
                    act.wait_ge(gate_ready, n + 1)
                    at_least(act, hidden_ready, n - 1)
                    nc.scalar.activation(gated[c % 2][:], gate[c % 2][:], ACT.Silu).then_inc(gated_ready, 1)
                    if c == 6 and not is_last(g, GROUPS):
                        at_least(act, up_ready, HC * g)
                        f.take_high(g + 1, 1 - slot)
            pipelined(act, step, GROUPS)

        @block.vector
        def _(dve):
            dve.wait_ge(r_loaded, 16)
            dve.wait_ge(consts, 3)
            nc.vector.tensor_copy(r_high[:], r_f[:]).then_inc(w_split, 1)
            dve.wait_ge(w_split, 1)
            nc.vector.tensor_tensor(r_low[:], r_f[:], r_high[:].bitcast(F32), ALU.subtract).then_inc(w_split, 1)
            f.normalise(0, 0)
            f.take_low(0, 0)
            for c in range(CHUNKS):
                s = slice(c * WC, (c + 1) * WC)
                dve.wait_ge(w_loaded[c % 2], 32 * (c // 2 + 1))
                nc.vector.tensor_copy(w_high[:, s], w_f[c % 2][:]).then_inc(w_split, 1)
                dve.wait_ge(w_split, 2 * c + 3)
                nc.vector.tensor_tensor(w_low[:, s], w_f[c % 2][:], w_high[:, s].bitcast(F32), ALU.subtract).then_inc(w_split, 1)

            def collect(g, slot, c):
                n = HC * g + c
                if c == EXPERTS:
                    return
                waits_apart(dve, (down_done, n + 1), (out_read, EXPERTS * g + min(c, EXPERTS)))
                if c == CHUNKS - 1:
                    nc.vector.tensor_tensor(f.resid[slot][:], f.resid[slot][:], out[:], ALU.add).then_inc(y_ready, 1)
                    return
                for t in range(GT):
                    ins = nc.vector.scalar_tensor_tensor(f.resid[slot][:, t, :], out[:, t, :], router.cw[slot][:, t, c:c + 1], f.resid[slot][:, t, :],
                                                         ALU.mult, ALU.add)
                ins.then_inc(out_read, 1)

            def step(g, slot):
                router.choose(g, slot)
                for c in range(HC):
                    n = g * HC + c
                    dve.wait_ge(gated_ready, n + 1)
                    dve.wait_ge(up_ready, n + 1)
                    at_least(dve, h_low_ready, n - 1)
                    nc.vector.tensor_tensor(hidden[c % 2][:], gated[c % 2][:], up[c % 2][:], ALU.mult).then_inc(hidden_ready, 1)
                    if c >= 2:
                        collect(g, slot, c - 2)
                    elif not is_first(g):
                        collect(g - 1, 1 - slot, HC - 2 + c)
                    if c == 2 and not is_last(g, GROUPS):
                        f.normalise(g + 1, 1 - slot, [(y_ready, g), (y_stored[1 - slot], 8 * (g + slot))])
                    if c == 7 and not is_last(g, GROUPS):
                        f.take_low(g + 1, 1 - slot)
            pipelined(dve, step, GROUPS)
            collect(GROUPS - 1, 1, HC - 2)
            collect(GROUPS - 1, 1, HC - 1)

        @block.tensor
        def _(pe):
            pe.wait_ge(consts, 2)
            f.turn(0, identity[:])

            def down_chunk(g, c):
                n = HC * g + c
                pe.wait_ge(h_low_ready, n + 1)
                if c == 0:
                    at_least(pe, y_ready, g)
                elif c <= EXPERTS:
                    pe.wait_ge(out_read, EXPERTS * g + c)
                for t in range(GT):
                    ts = slice(t * P, (t + 1) * P)
                    ins = product(nc, out[:, t, :], [(h_high[:, c % RING, ts], h_low[:, c % RING, ts], *w2(c))],
                                  start=(c <= EXPERTS and t % 2 == 0), stop=(c != EXPERTS), shared=True)
                ins.then_inc(down_done, 1)

            def step(g, slot):
                pe.wait_ge(f.low_ready, g + 1)
                for t in range(GT):
                    ts = slice(t * P, (t + 1) * P)
                    ins = product(nc, turned[:, 0, t * EXPERTS:(t + 1) * EXPERTS],
                                  [(f.high[slot][:, k, ts], f.low[slot][:, k, ts], r_high[:, k * EXPERTS:(k + 1) * EXPERTS], r_low[:, k * EXPERTS:(k + 1) * EXPERTS])
                                   for k in range(KC)])
                ins.then_inc(router.logits_ready, 1)
                for c in range(HC):
                    n = g * HC + c
                    if is_first(g):
                        pe.wait_ge(w_split, 2 * c + 4)
                    at_least(pe, hidden_ready, n - 1)
                    for bank, kind, ready in ((gate, 0, gate_ready), (up, 1, up_ready)):
                        product(nc, bank[c % 2][:], [(*w1(c, kind, k), f.high[slot][:, k, :], f.low[slot][:, k, :])
                                                     for k in range(KC)]).then_inc(ready, 1)
                    if c >= 2:
                        down_chunk(g, c - 2)
                    elif not is_first(g):
                        down_chunk(g - 1, HC - 2 + c)
                    if c == 5 and not is_last(g, GROUPS):
                        pe.wait_ge(router.chain, Router.STEPS * g + 2)
                        f.turn(g + 1, identity[:])
            pipelined(pe, step, GROUPS)
            down_chunk(GROUPS - 1, HC - 2)
            down_chunk(GROUPS - 1, HC - 1)


def rope_tables():
    f = (1.0 / 10000.0 ** (np.arange(0, HD, 2, dtype=np.float32) / HD)).astype(np.float32)
    a = np.arange(SEQ, dtype=np.float32)[:, None] * f[None, :]
    return np.cos(a).astype(np.float32), np.concatenate([-np.sin(a), np.sin(a)], axis=1).astype(np.float32)


def even_first(w):
    return w.reshape(D, HEADS, HALF, 2).transpose(0, 1, 3, 2).reshape(D, D)


def build(nc, inputs, out):
    scratch = lambda n, s, d=F32: nc.dram_tensor(n, s, d, kind="Internal").ap()
    qk = scratch("qk", (UNITS, QK * PARTS, HG * HD, SEQ), BF16)
    v = scratch("v", (UNITS, SEQ, HG * VW))
    att = scratch("att", (UNITS, P, SEQ))
    x1, x2, x3 = (scratch(f"x{i}", (TOKENS, D)) for i in (1, 2, 3))
    rope_qkv(nc, inputs["x"], inputs["w_qkv0"], inputs["cos"], inputs["sin"], qk, v)
    causal_attention(nc, qk, v, att)
    attention_out(nc, inputs["x"], att, inputs["w_o"], x1)
    swiglu_ffn(nc, x1, inputs["gate_up0"], inputs["down0"], x2)
    column_attention(nc, x2, inputs["w_qkv1"], x3)
    experts(nc, x3, inputs["w_router"], inputs["gate_up1"], inputs["down1"], out)


def kernel(L0_attn_x, L0_attn_qw, L0_attn_kw, L0_attn_vw, L0_attn_ow, L0_ffn_w_gate, L0_ffn_w_up, L0_ffn_w_down,
           L1_attn_W_query, L1_attn_W_key, L1_attn_W_value, L1_ffn_Wr, L1_ffn_Wg, L1_ffn_Wu, L1_ffn_Wd,
           L1_ffn_Sg, L1_ffn_Su, L1_ffn_Sd):
    import concourse.bacc as bacc
    from concourse.bass_utils import run_bass_kernel_spmd

    cat = lambda *a, axis: np.ascontiguousarray(np.concatenate(a, axis=axis))
    cos, sin = rope_tables()
    chunked = lambda w: w.reshape(D, 2, P).transpose(1, 0, 2)
    arrays = {
        "x": np.ascontiguousarray(L0_attn_x).reshape(TOKENS, D),
        "w_qkv0": cat(even_first(L0_attn_qw), even_first(L0_attn_kw), L0_attn_vw, axis=1),
        "cos": cos, "sin": sin,
        "w_o": np.ascontiguousarray(L0_attn_ow),
        "gate_up0": cat(L0_ffn_w_gate.T, L0_ffn_w_up.T, axis=1),
        "down0": np.ascontiguousarray(L0_ffn_w_down.T),
        "w_qkv1": cat(L1_attn_W_query, L1_attn_W_key, L1_attn_W_value, axis=1),
        "w_router": np.ascontiguousarray(L1_ffn_Wr),
        "gate_up1": cat(cat(L1_ffn_Wg, L1_ffn_Wu, axis=2), cat(chunked(L1_ffn_Sg), chunked(L1_ffn_Su), axis=2), axis=0),
        "down1": cat(L1_ffn_Wd.reshape(EXPERTS * P, D), L1_ffn_Sd, axis=0),
    }
    nc = bacc.Bacc("TRN2", target_bir_lowering=False, num_devices=1)
    inputs = {n: nc.dram_tensor(n, a.shape, mybir.dt.from_np(a.dtype), kind="ExternalInput").ap() for n, a in arrays.items()}
    out = nc.dram_tensor("out", (TOKENS, D), F32, kind="ExternalOutput").ap()
    build(nc, inputs, out)
    result = run_bass_kernel_spmd(nc, [arrays], core_ids=[0])
    return result.results[0]["out"].reshape(BATCH, SEQ, D)
```

```python
from contextlib import ExitStack

import numpy as np

import concourse.bass as bass
from concourse import mybir

F32 = mybir.dt.float32
F32R = mybir.dt.float32r
BF16 = mybir.dt.bfloat16
I32 = mybir.dt.int32
U32 = mybir.dt.uint32
ACT = mybir.ActivationFunctionType
ALU = mybir.AluOpType
AX_X = mybir.AxisListType.X

P = 128
BATCH, SEQ, D = 8, 1024, 256
TOKENS = BATCH * SEQ
KC = D // P
GT = 4
GN = GT * P
GROUPS = TOKENS // GN
EPS = 1e-5
NEWTON = 3
ROOT_STEPS = 2 + 3 * NEWTON
FRONT_STEPS = 2 * GT + ROOT_STEPS


def at_least(engine, semaphore, value):
    if not (isinstance(value, int) and value <= 0):
        engine.wait_ge(semaphore, value)


def waits_apart(engine, *waits):
    waits = [(s, v if isinstance(v, int) else engine.to_reg(v)) for s, v in waits]
    if not isinstance(waits[-1][1], int):
        engine.wait_ge(waits[0][0], 1)
    for semaphore, value in waits:
        at_least(engine, semaphore, value)


def pipelined(engine, step, count, ways=2):
    for i in range(ways):
        step(i, i)
    with engine.Fori(1, count // ways - 1) as turn:
        for k in range(ways):
            step(ways * turn + k, k)
    for k in range(ways):
        step(count - ways + k, k)


def is_first(i):
    return isinstance(i, int) and i == 0


def is_last(i, count):
    return isinstance(i, int) and i == count - 1


def group_rows(x, g):
    return x[bass.ds(g * GN, GN), :].rearrange("(t p) d -> p t d", p=P)


def fill_identity(nc, identity, done):
    nc.gpsimd.memset(identity[:], 0.0).then_inc(done, 1)
    nc.gpsimd.wait_ge(done, 1)
    nc.gpsimd.affine_select(out=identity[:], in_=identity[:], compare_op=ALU.not_equal, fill=1.0, base=0,
                            pattern=[[-1, P]], channel_multiplier=1).then_inc(done, 1)


class Front:

    def __init__(self, nc, ctx, tag, turned):
        sb = lambda n, s, d: ctx.enter_context(nc.sbuf_tensor(f"{tag}_{n}", s, d))
        sem = lambda n: ctx.enter_context(nc.semaphore(f"{tag}_{n}"))
        self.nc = nc
        self.x = [sb(f"x{i}", [P, GT, D], F32) for i in range(2)]
        self.resid = [sb(f"resid{i}", [P, GT, D], F32) for i in range(2)]
        self.xn = sb("xn", [P, GT, D], F32)
        self.stats = sb("stats", [P, GT, 6], F32)
        self.moments = sb("moments", [P, GT, 2], F32)
        self.variance = sb("variance", [P, GT], F32)
        self.rstd = sb("rstd", [P, GT], F32)
        self.root_t = sb("root_t", [P, GT], F32)
        self.high = [sb(f"high{i}", [P, KC, GN], F32R) for i in range(2)]
        self.low = [sb(f"low{i}", [P, KC, GN], F32R) for i in range(2)]
        self.turned = turned
        self.x_loaded = [sem("x_loaded_even"), sem("x_loaded_odd")]
        self.stats_done = sem("stats_done")
        self.xn_ready = sem("xn_ready")
        self.turned_ready = sem("turned_ready")
        self.high_ready = sem("high_ready")
        self.low_ready = sem("low_ready")

    def load(self, x_in, g, slot):
        at_least(self.nc.sync, self.xn_ready, g - 1)
        self.nc.sync.dma_start(self.x[slot][:], group_rows(x_in, g)).then_inc(self.x_loaded[slot], 16)

    def normalise(self, g, slot, resid_free=(), keep=True):
        self.take_moments(g, slot, resid_free, keep)
        self.root(g)
        self.scale(g, slot)

    def take_moments(self, g, slot, resid_free=(), keep=True):
        dve, x = self.nc.vector, self.x[slot]
        steps = FRONT_STEPS
        dve.wait_ge(self.x_loaded[slot], 8 * g + 16 - 8 * slot)
        for t in range(GT):
            dve.bn_stats(self.stats[:, t, :], x[:, t, :]).then_inc(self.stats_done, 1)
        for semaphore, value in resid_free:
            at_least(dve, semaphore, value)
        if keep:
            dve.tensor_copy(self.resid[slot][:], x[:])
        waits_apart(dve, (self.stats_done, steps * g + GT))
        for t in range(GT):
            dve.bn_aggr(self.moments[:, t, :], self.stats[:, t, :]).then_inc(self.stats_done, 1)

    def root(self, g):
        self.nc.vector.wait_ge(self.stats_done, FRONT_STEPS * g + 2 * GT)
        self.inverse_root(FRONT_STEPS * g + 2 * GT)

    def scale(self, g, slot):
        dve, x = self.nc.vector, self.x[slot]
        at_least(dve, self.turned_ready, g)
        for t in range(GT):
            ins = dve.tensor_scalar(self.xn[:, t, :], x[:, t, :], self.moments[:, t, 0:1], self.rstd[:, t:t + 1],
                                    ALU.subtract, ALU.mult)
        ins.then_inc(self.xn_ready, 1)

    def inverse_root(self, done):
        dve, v, y, t = self.nc.vector, self.variance, self.rstd, self.root_t
        ops = [lambda: dve.tensor_scalar(v[:], self.moments[:, :, 1], EPS, None, ALU.add),
               lambda: dve.tensor_scalar(y[:].bitcast(I32), v[:].bitcast(I32), -0.5, float(0x5F3759DF), ALU.mult, ALU.add)]
        for _ in range(NEWTON):
            ops += [lambda: dve.tensor_tensor(t[:], y[:], y[:], ALU.mult),
                    lambda: dve.scalar_tensor_tensor(t[:], t[:], -0.5, v[:], ALU.mult, ALU.mult),
                    lambda: dve.scalar_tensor_tensor(y[:], t[:], 1.5, y[:], ALU.add, ALU.mult)]
        for n, op in enumerate(ops):
            op().then_inc(self.stats_done, 1)
            dve.wait_ge(self.stats_done, done + n + 1)

    def turn(self, g, identity):
        pe = self.nc.tensor
        pe.wait_ge(self.xn_ready, g + 1)
        at_least(pe, self.low_ready, g)
        for c in range(KC):
            for t in range(GT):
                ins = pe.transpose(self.turned[:, c, t * P:(t + 1) * P], self.xn[:, t, c * P:(c + 1) * P], identity)
        ins.then_inc(self.turned_ready, 1)

    def take_high(self, g, slot):
        self.nc.scalar.wait_ge(self.turned_ready, g + 1)
        self.nc.scalar.copy(self.high[slot][:], self.turned[:]).then_inc(self.high_ready, 1)

    def take_low(self, g, slot):
        dve = self.nc.vector
        dve.wait_ge(self.high_ready, g + 1)
        dve.tensor_tensor(self.low[slot][:], self.turned[:], self.high[slot][:].bitcast(F32),
                          ALU.subtract).then_inc(self.low_ready, 1)


def product(nc, out, pairs, start=True, stop=True, shared=False):
    passes = [(w, m) for wh, wl, mh, ml in pairs for w, m in ((wh, mh), (wl, mh), (wh, ml)) if w is not None and m is not None]
    for n, (w, m) in enumerate(passes):
        ins = nc.tensor.matmul(out, w, m, start=start and n == 0, stop=stop and n == len(passes) - 1,
                               skip_group_check=shared)
    return ins
HEADS = 16
HD = D // HEADS
HALF = HD // 2
HG = 4
UNITS = BATCH * HEADS // HG
PARTS = 3
QK = 2
VW = 32
QBLOCKS = SEQ // P
TILES = TOKENS // P


def rope_qkv(nc, x_in, w_qkv, cos, sin, qk_out, v_out):
    with ExitStack() as ctx:
        sb = lambda n, s, d: ctx.enter_context(nc.sbuf_tensor(f"qkv_{n}", s, d))
        ps = lambda n, s, d=F32: ctx.enter_context(nc.psum_tensor(f"qkv_{n}", s, d))
        sem = lambda n: ctx.enter_context(nc.semaphore(f"qkv_{n}"))
        W = KC * 3 * D
        w_f = sb("w_f", [P, W], F32)
        w_high = sb("w_high", [P, W], F32R)
        w_low = sb("w_low", [P, W], F32R)
        identity = sb("identity", [P, P], F32)
        identity16 = sb("identity16", [P, P], BF16)
        cos_t = sb("cos", [P, QBLOCKS, HALF], F32)
        sin_t = sb("sin", [P, QBLOCKS, 2, HALF], F32)
        RING = GT
        by_cos = [sb(f"by_cos{i}", [P, QK * D], F32) for i in range(2)]
        by_sin = [sb(f"by_sin{i}", [P, QK * D], F32) for i in range(2)]
        r = [sb(f"r{i}", [P, QK * D], F32) for i in range(RING)]
        rest = [sb(f"rest{i}", [P, QK * D], F32) for i in range(RING)]
        parts = [sb(f"parts{i}", [P, PARTS, QK * D], BF16) for i in range(RING)]
        stage = [sb(f"stage{i}", [P, QK * PARTS, KC, GN], BF16) for i in range(2)]
        v_stage = [sb(f"v_stage{i}", [P, GT, HEADS, VW], F32) for i in range(2)]
        turned = ps("turned", [P, KC, GN])
        qk = [ps(f"qk{i}", [P, QK * D]) for i in range(2)]
        v = [ps(f"v{i}", [P, D]) for i in range(2)]
        across = [ps(f"across{i}", [P, PARTS * KC, P], BF16) for i in range(QK)]
        f = Front(nc, ctx, "qkv", turned)
        w_loaded, w_ready, consts = sem("w_loaded"), sem("w_ready"), sem("consts")
        qk_ready, v_ready = sem("qk_ready"), sem("v_ready")
        rope_ready = sem("rope_ready")
        r_ready, rest_ready = sem("r_ready"), sem("rest_ready")
        v_taken, first_ready, second_ready = sem("v_taken"), sem("first_ready"), sem("second_ready")
        third_ready = sem("third_ready")
        across_ready = sem("across_ready")
        q_taken, k_taken = sem("q_taken"), sem("k_taken")
        stored = [sem("stored_even"), sem("stored_odd")]
        v_stored = [sem("v_stored_even"), sem("v_stored_odd")]
        STORES = HEADS // HG

        block = ctx.enter_context(nc.Block())

        def lagged(n, lag):
            return not isinstance(n, int) or 0 <= n - lag < TILES

        @block.sync
        def _(sp):
            f.load(x_in, 0, 0)
            sp.dma_start(w_f[:].rearrange("p (c n) -> p c n", c=KC), w_qkv.rearrange("(c p) n -> p c n", p=P)).then_inc(w_loaded, 16)
            sp.dma_start(cos_t[:], cos.rearrange("(t p) e -> p t e", p=P)).then_inc(w_loaded, 16)
            sp.dma_start(sin_t[:], sin.rearrange("(t p) (s e) -> p t s e", p=P, s=2)).then_inc(w_loaded, 16)
            f.load(x_in, 1, 1)

            def store_qk(g, slot, b):
                sp.wait_ge(q_taken, GT * (g + 1))
                sp.wait_ge(k_taken, GT * (g + 1))
                for side in range(2):
                    for c in range(KC):
                        out = qk_out[bass.ds(b * (HEADS // HG) + 2 * c + side, 1), :, :, slot * GN:(slot + 1) * GN]
                        sp.dma_start(out.rearrange("u a p n -> p (u a) n"),
                                     stage[slot][64 * side:64 * side + 64, :, c, :]).then_inc(stored[slot], 16)

            def store_v(g, slot, b):
                sp.wait_ge(v_taken, GT * (g + 1))
                for unit in range(HEADS // HG):
                    out = v_out[bass.ds(b * (HEADS // HG) + unit, 1), slot * GN:(slot + 1) * GN, :]
                    sp.dma_start(out.rearrange("u (t p) n -> p (u t) n", p=P),
                                 v_stage[slot][:, :, unit * HG:(unit + 1) * HG, :].rearrange("p t h n -> p t (h n)")).then_inc(v_stored[slot], 16)

            def pair(b):
                if not is_last(b, BATCH):
                    f.load(x_in, 2 * b + 2, 0)
                if not is_first(b):
                    store_qk(2 * b - 1, 1, b - 1)
                store_v(2 * b, 0, b)
                if not is_last(b, BATCH):
                    f.load(x_in, 2 * b + 3, 1)
                store_qk(2 * b, 0, b)
                store_v(2 * b + 1, 1, b)
            pair(0)
            with sp.Fori(1, BATCH - 1) as b:
                pair(b)
            pair(BATCH - 1)
            store_qk(GROUPS - 1, 1, BATCH - 1)
            for s in stored + v_stored:
                sp.wait_ge(s, 16 * STORES * GROUPS // 2)

        @block.gpsimd
        def _(pool):
            fill_identity(nc, identity, consts)
            pool.wait_ge(consts, 2)
            nc.gpsimd.tensor_copy(identity16[:], identity[:]).then_inc(consts, 1)
            for s in v_stage:
                nc.gpsimd.memset(s[:], 0.0).then_inc(consts, 1)
            pool.wait_ge(consts, 5)
            for s in v_stage:
                nc.gpsimd.memset(s[:, :, :, HD:HD + 1], 1.0).then_inc(consts, 1)

            def tile(n, t):
                if lagged(n, 1):
                    s = (t - 1) % RING
                    at_least(pool, third_ready, n - 4)
                    pool.wait_ge(first_ready, n)
                    nc.gpsimd.tensor_tensor(rest[s][:], r[s][:], parts[s][:, 0, :], ALU.subtract).then_inc(rest_ready, 1)
                if lagged(n, 0):
                    at_least(pool, first_ready, n - 3)
                    at_least(pool, rest_ready, n - 3)
                    pool.wait_ge(rope_ready, n + 1)
                    nc.gpsimd.tensor_tensor(r[t][:], by_cos[t % 2][:], by_sin[t % 2][:], ALU.add).then_inc(r_ready, 1)
            pipelined(pool, lambda g, slot: [tile(GT * g + t, t) for t in range(GT)], GROUPS)
            tile(TILES, 0)

        @block.scalar
        def _(act):
            f.take_high(0, 0)

            def tile(n, t, slot, g=None):
                if lagged(n, 0):
                    act.wait_ge(v_ready, n + 1)
                    if t == 0:
                        at_least(act, v_stored[slot], 2 * STORES * n - 8 * STORES * slot)
                        if isinstance(n, int) and n < 2 * GT:
                            act.wait_ge(consts, 7)
                    nc.scalar.copy(v_stage[slot][:, t, :, 0:HD], v[t % 2][:].rearrange("p (h e) -> p h e", h=HEADS)).then_inc(v_taken, 1)
                if lagged(n, 1):
                    s = (t - 1) % RING
                    act.wait_ge(rest_ready, n)
                    nc.scalar.copy(parts[s][:, 1, :], rest[s][:]).then_inc(second_ready, 1)
                if lagged(n, 3):
                    s = (t - 3) % GT
                    at = slot if t >= 3 else 1 - slot
                    act.wait_ge(across_ready, n - 2)
                    if s == 0:
                        at_least(act, stored[at], 2 * STORES * (n - 3) - 8 * STORES * at)
                    nc.scalar.copy(stage[at][:, 0:PARTS, :, s * P:(s + 1) * P],
                                   across[0][:].rearrange("p (a c) n -> p a c n", c=KC)).then_inc(q_taken, 1)
                    nc.scalar.copy(stage[at][:, PARTS:2 * PARTS, :, s * P:(s + 1) * P],
                                   across[1][:].rearrange("p (a c) n -> p a c n", c=KC)).then_inc(k_taken, 1)
                if t == 2 and g is not None and not is_last(g, GROUPS):
                    at_least(act, v_ready, GT * g)
                    f.take_high(g + 1, 1 - slot)
                if lagged(n, 0):
                    at_least(act, across_ready, n - 3)
                    act.wait_ge(r_ready, n + 1)
                    nc.scalar.copy(parts[t][:, 0, :], r[t][:]).then_inc(first_ready, 1)

            def step(g, slot):
                for t in range(GT):
                    tile(GT * g + t, t, slot, g)
            pipelined(act, step, GROUPS)
            for t in range(3):
                tile(TILES + t, t, 0)

        @block.vector
        def _(dve):
            f.normalise(0, 0, keep=False)
            dve.wait_ge(w_loaded, 48)
            nc.vector.tensor_copy(w_high[:], w_f[:]).then_inc(w_ready, 1)
            dve.wait_ge(w_ready, 1)
            nc.vector.tensor_tensor(w_low[:], w_f[:], w_high[:].bitcast(F32), ALU.subtract).then_inc(w_ready, 1)
            f.take_low(0, 0)

            def tile(n, t, slot):
                if lagged(n, 0):
                    where = slot * GT + t
                    dve.wait_ge(qk_ready, n + 1)
                    at_least(dve, r_ready, n - 1)
                    x = qk[t % 2][:].rearrange("p (h s e) -> p h s e", s=2, e=HALF)
                    c = cos_t[:, where:where + 1, :].broadcast_to([P, 2 * QK * HEADS, HALF])
                    nc.vector.tensor_tensor(by_cos[t % 2][:].rearrange("p (h e) -> p h e", e=HALF),
                                            qk[t % 2][:].rearrange("p (h e) -> p h e", e=HALF), c, ALU.mult)
                    out = by_sin[t % 2][:].rearrange("p (h s e) -> p h s e", s=2, e=HALF)
                    for s in range(2):
                        w = sin_t[:, where, s:s + 1, :].broadcast_to([P, QK * HEADS, HALF])
                        ins = nc.vector.tensor_tensor(out[:, :, s, :], x[:, :, 1 - s, :], w, ALU.mult)
                    ins.then_inc(rope_ready, 1)
                if lagged(n, 2):
                    s = (t - 2) % RING
                    dve.wait_ge(second_ready, n - 1)
                    nc.vector.tensor_tensor(parts[s][:, 2, :], rest[s][:], parts[s][:, 1, :], ALU.subtract).then_inc(third_ready, 1)

            def step(g, slot):
                for t in range(GT):
                    if t == 3 and not is_last(g, GROUPS):
                        f.take_low(g + 1, 1 - slot)
                    if not is_last(g, GROUPS):
                        if t == 0:
                            f.take_moments(g + 1, 1 - slot, keep=False)
                        if t == 1:
                            f.root(g + 1)
                        if t == 2:
                            f.scale(g + 1, 1 - slot)
                    tile(GT * g + t, t, slot)
            pipelined(dve, step, GROUPS)
            for t in range(3):
                tile(TILES + t, t, 0)

        @block.tensor
        def _(pe):
            pe.wait_ge(consts, 3)
            f.turn(0, identity[:])
            pe.wait_ge(w_ready, 2)

            def tile(n, t, slot):
                if lagged(n, 0):
                    at_least(pe, rope_ready, n - 1)
                    at_least(pe, v_taken, n - 1)
                    ts = slice(t * P, (t + 1) * P)
                    for bank, at, width, ready in ((qk, 0, QK * D, qk_ready), (v, QK * D, D, v_ready)):
                        cols = [slice(k * 3 * D + at, k * 3 * D + at + width) for k in range(KC)]
                        product(nc, bank[t % 2][:], [(f.high[slot][:, k, ts], f.low[slot][:, k, ts], w_high[:, cols[k]], w_low[:, cols[k]])
                                                     for k in range(KC)]).then_inc(ready, 1)
                if lagged(n, 3):
                    s = (t - 3) % RING
                    pe.wait_ge(third_ready, n - 2)
                    at_least(pe, q_taken, n - 3)
                    at_least(pe, k_taken, n - 3)
                    for i in range(QK):
                        for a in range(PARTS):
                            for c in range(KC):
                                ins = nc.tensor.transpose(across[i][:, a * KC + c, :], parts[s][:, a, i * D + c * P:i * D + (c + 1) * P], identity16[:])
                    ins.then_inc(across_ready, 1)

            def step(g, slot):
                pe.wait_ge(f.low_ready, g + 1)
                for t in range(GT):
                    tile(GT * g + t, t, slot)
                    if t == 2 and not is_last(g, GROUPS):
                        f.turn(g + 1, identity[:])
            pipelined(pe, step, GROUPS)
            for t in range(3):
                tile(TILES + t, t, 0)


STEPS = [(c, j) for c in range(2) for j in range(4 * c + 4)]
NSTEP = len(STEPS)
PIECES = [(i, lo) for i in range(QBLOCKS) for lo in range(0, (i + 1) * P, GN)]
NP_HEAD = len(PIECES)
NP_UNIT = HG * NP_HEAD
COMBOS = ((0, 0), (0, 1), (0, 2), (1, 0), (1, 1), (2, 0))
ROWS = len(COMBOS) * HD
LOW = -1e30
WAYS = 4
E_RING = 6
QUERY_SCALE = float(HD) ** -0.5


def causal_attention(nc, qk_in, v_in, o_out):
    with ExitStack() as ctx:
        sb = lambda n, s, d: ctx.enter_context(nc.sbuf_tensor(f"att_{n}", s, d))
        ps = lambda n, s, d=F32: ctx.enter_context(nc.psum_tensor(f"att_{n}", s, d))
        sem = lambda n: ctx.enter_context(nc.semaphore(f"att_{n}"))
        q = [sb(f"q{i}", [P, HG, SEQ], BF16) for i in range(WAYS)]
        k = [sb(f"k{i}", [P, HG, SEQ], BF16) for i in range(WAYS)]
        v = [sb(f"v{i}", [P, QBLOCKS, HG * VW], F32) for i in range(WAYS)]
        e = [sb(f"e{i}", [P, HG, GN], F32) for i in range(E_RING)]
        o = [sb(f"o{i}", [P, GN], F32) for i in range(2)]
        identity = sb("identity", [P, P], F32)
        identity16 = sb("identity16", [P, P], BF16)
        mask = sb("mask", [P, GN], F32)
        unused = [sb(f"unused{i}", [P, GN], F32) for i in range(3)]
        tops = sb("tops", [P, HG, QBLOCKS], F32)
        tops0 = sb("tops0", [P, HG, QBLOCKS // 2], F32)
        rest = sb("rest", [P, HG, QBLOCKS], F32)
        minus = sb("minus", [P, PARTS, HG, QBLOCKS], BF16)
        rows = sb("rows", [PARTS * HG * QBLOCKS, P], BF16)
        by_key = [ps(f"by_key{i}", [P, 2, GN]) for i in range(2)]
        by_query = [ps(f"by_query{i}", [P, GN]) for i in range(3)]
        total = ps("total", [P, GN])
        consts, loaded, v_loaded = sem("consts"), [sem(f"loaded{i}") for i in range(WAYS)], [sem(f"v_loaded{i}") for i in range(WAYS)]
        query_ready, query_read = sem("query_ready"), sem("query_read")
        split = sem("split")
        rows_turned, rows_taken, rows_placed = sem("rows_turned"), sem("rows_taken"), sem("rows_placed")
        key_ready, weights_ready = sem("key_ready"), sem("weights_ready")
        masked = sem("masked")
        summed = sem("summed")
        o_taken = sem("o_taken")
        o_stored = [sem("o_stored0"), sem("o_stored1")]
        SPLITS = 5
        LOADS = QK * len(COMBOS)
        DIAGONAL = 8
        AHEAD = 14
        TURN_AT = 6
        LAG = 4

        block = ctx.enter_context(nc.Block())

        def diagonal(s):
            c, j = STEPS[s]
            return j >= 4 * c

        def offset(s):
            c, j = STEPS[s]
            return max(0, j - 4 * c) * P

        def shares():
            parts = []
            for s in range(NSTEP):
                w = (s - LAG) % NSTEP
                parts += [2 * (GN - offset(s)) + 128, 2 * (GN - offset(s)) + 128, 3 * (GN - offset(w)) + 128]
            order = [m % NP_UNIT for m in range(AHEAD, AHEAD + NP_UNIT)]
            costs = [min((i + 1) * P - lo, GN) + 128 for i, lo in (PIECES[m % NP_HEAD] for m in order)]
            share, n = [0], 0
            for k in range(len(parts)):
                while n < NP_UNIT and sum(costs[:n]) * sum(parts) < sum(parts[:k + 1]) * sum(costs):
                    n += 1
                share.append(n)
            return share

        SHARE = shares()

        def diagonals_to(s):
            return sum(diagonal(i) for i in range(s + 1))

        @block.sync
        def _(sp):
            def load(u, way):
                for i, stack in enumerate((q, k)):
                    for n, combo in enumerate(COMBOS):
                        a = i * PARTS + combo[i]
                        src = qk_in[bass.ds(u, 1), a, :, :].rearrange("u (j d) n -> d (u j) n", d=HD)
                        sp.dma_start(stack[way][n * HD:(n + 1) * HD, :, :], src).then_inc(loaded[way], 16)
                sp.dma_start(v[way][:], v_in[bass.ds(u, 1), :, :].rearrange("u (t p) n -> p (u t) n", p=P)).then_inc(v_loaded[way], 16)

            def place(u, way):
                sp.wait_ge(rows_taken, u + 1)
                n = HG * QBLOCKS
                for a in range(PARTS):
                    sp.dma_start(q[way][ROWS + a:ROWS + a + 1, :, :].rearrange("a j (i n) -> a (j i) n", n=P),
                                 rows[a * n:(a + 1) * n, :]).then_inc(rows_placed, 16)

            def store(u, c):
                sp.wait_ge(o_taken, 2 * u + c + 1)
                sp.dma_start(o_out[bass.ds(u, 1), :, c * GN:(c + 1) * GN].rearrange("u p n -> p (u n)"), o[c][:]).then_inc(o_stored[c], 16)
            load(0, 0)
            load(1, 1)
            place(0, 0)
            load(2, 2)

            def step(u, way):
                if not is_first(u):
                    store(u - 1, 1)
                if not (isinstance(u, int) and u + 3 >= UNITS):
                    at_least(sp, summed, NSTEP * u)
                    load(u + 3, (way + 3) % WAYS)
                store(u, 0)
                if not is_last(u, UNITS):
                    place(u + 1, (way + 1) % WAYS)
            pipelined(sp, step, UNITS, WAYS)
            store(UNITS - 1, 1)
            for s in o_stored:
                sp.wait_ge(s, 16 * UNITS)

        @block.gpsimd
        def _(pool):
            fill_identity(nc, identity, consts)
            pool.wait_ge(consts, 2)
            nc.gpsimd.tensor_copy(identity16[:], identity[:]).then_inc(consts, 1)
            nc.gpsimd.memset(mask[:], 0.0).then_inc(consts, 1)
            pool.wait_ge(consts, 4)
            last = mask[:, GN - P:GN]
            nc.gpsimd.affine_select(out=last, in_=last, compare_op=ALU.is_ge, fill=LOW, base=0,
                                    pattern=[[-1, P]], channel_multiplier=1).then_inc(consts, 1)
            for i, s in enumerate(k):
                pool.wait_ge(consts, 5 + i)
                nc.gpsimd.memset(s[ROWS:P, :, :], 1.0).then_inc(consts, 1)

            def step(u, way):
                for s in range(NSTEP):
                    if diagonal(s):
                        waits_apart(pool, (weights_ready, 2 * (NSTEP * u + s + 1)))
                        w = e[s % E_RING][:, :, offset(s):offset(s) + P]
                        nc.gpsimd.affine_select(out=w, in_=w, compare_op=ALU.is_ge, fill=0.0, base=0,
                                                pattern=[[0, HG], [1, P]], channel_multiplier=-1).then_inc(masked, 1)
            pipelined(pool, step, UNITS, WAYS)

        @block.scalar
        def _(act):
            def take(u, c):
                act.wait_ge(summed, NSTEP * u + (4 if c == 0 else NSTEP))
                at_least(act, o_stored[c], 16 * u)
                nc.scalar.copy(o[c][:], total[:]).then_inc(o_taken, 1)

            def step(u, way):
                for s in range(NSTEP):
                    if s == LAG and not is_first(u):
                        take(u - 1, 1)
                    if s == 4 + LAG:
                        take(u, 0)
                    for pair in range(2):
                        n = 2 * (NSTEP * u + s) + pair
                        act.wait_ge(key_ready, n + 1)
                        if pair == 0:
                            at_least(act, summed, NSTEP * u + s - E_RING + 1)
                        nc.scalar.activation(e[s % E_RING][:, 2 * pair:2 * pair + 2, offset(s):GN],
                                             by_key[pair][:, :, offset(s):GN], ACT.Exp, scale=QUERY_SCALE).then_inc(weights_ready, 1)
            pipelined(act, step, UNITS, WAYS)
            take(UNITS - 1, 1)

        @block.vector
        def _(dve):
            def piece(u, way, m):
                h, n = m // NP_HEAD, m % NP_HEAD
                i, lo = PIECES[n]
                bank = by_query[m % 3]
                width = min((i + 1) * P - lo, GN)
                waits_apart(dve, (query_ready, NP_UNIT * u + m + 1))
                if lo + GN <= i * P:
                    ins = nc.vector.tensor_reduce(tops0[:, h, i - 4:i - 3], bank[:], AX_X, ALU.max)
                else:
                    ins = nc.vector.tensor_tensor_reduce(unused[m % 3][:, 0:width], bank[:, 0:width], mask[:, GN - width:GN],
                                                         1.0, 3 * LOW, ALU.add, ALU.max, tops[:, h, i:i + 1])
                ins.then_inc(query_read, 1)

            def split_maxima(u):
                at = SPLITS * u
                dve.wait_ge(query_read, NP_UNIT * (u + 1))
                nc.vector.tensor_tensor(tops[:, :, 4:8], tops[:, :, 4:8], tops0[:], ALU.max).then_inc(split, 1)
                dve.wait_ge(split, at + 1)
                at_least(dve, rows_turned, u)
                nc.vector.tensor_scalar(minus[:, 0], tops[:], -1.0, None, ALU.mult).then_inc(split, 1)
                dve.wait_ge(split, at + 2)
                nc.vector.scalar_tensor_tensor(rest[:], tops[:], -1.0, minus[:, 0], ALU.mult, ALU.subtract).then_inc(split, 1)
                dve.wait_ge(split, at + 3)
                nc.vector.tensor_copy(minus[:, 1], rest[:]).then_inc(split, 1)
                dve.wait_ge(split, at + 4)
                nc.vector.tensor_tensor(minus[:, 2], rest[:], minus[:, 1], ALU.subtract).then_inc(split, 1)

            def take_rows(u, way):
                dve.wait_ge(rows_turned, u + 1)
                at_least(dve, rows_placed, 48 * u)
                nc.vector.tensor_copy(rows[:], by_query[TURN_AT % 3][:].bitcast(BF16)[0:PARTS * HG * QBLOCKS, 0:P]).then_inc(rows_taken, 1)

            def step(u, way):
                for m in range(NP_UNIT):
                    if m == TURN_AT and not is_first(u):
                        take_rows(u - 1, (way - 1) % WAYS)
                    piece(u, way, m)
                split_maxima(u)
            dve.wait_ge(consts, 5)
            pipelined(dve, step, UNITS, WAYS)
            take_rows(UNITS - 1, WAYS - 1)

        @block.tensor
        def _(pe):
            def piece(u, way, m):
                h, (i, lo) = m // NP_HEAD, PIECES[m % NP_HEAD]
                if m == 0:
                    pe.wait_ge(loaded[way], LOADS * (u - way) * (16 // WAYS) + 16 * LOADS)
                if m == TURN_AT and not is_first(u):
                    at_least(pe, rows_taken, u)
                else:
                    at_least(pe, query_read, NP_UNIT * u + m - 2)
                width = min((i + 1) * P - lo, GN)
                nc.tensor.matmul(by_query[m % 3][:, 0:width], q[way][0:ROWS, h, i * P:(i + 1) * P],
                                 k[way][0:ROWS, h, lo:lo + width], start=True, stop=True).then_inc(query_ready, 1)

            def turn_rows(u, way):
                pe.wait_ge(split, SPLITS * (u + 1))
                if not is_last(u, UNITS):
                    pe.wait_ge(query_read, NP_UNIT * (u + 1) + TURN_AT - 2)
                nc.tensor.transpose(by_query[TURN_AT % 3][:].bitcast(BF16)[0:PARTS * HG * QBLOCKS, 0:P],
                                    minus[:].rearrange("p a h i -> p (a h i)"), identity16[:]).then_inc(rows_turned, 1)

            def scores(u, way, s, pair):
                c, j = STEPS[s]
                n = 2 * (NSTEP * u + s) + pair
                if s == 0 and pair == 0:
                    pe.wait_ge(rows_placed, 48 * (u + 1))
                at_least(pe, weights_ready, n - 1)
                for h in (2 * pair, 2 * pair + 1):
                    ins = nc.tensor.matmul(by_key[pair][:, h % 2, offset(s):GN], k[way][0:ROWS + PARTS, h, j * P:(j + 1) * P],
                                           q[way][0:ROWS + PARTS, h, c * GN + offset(s):(c + 1) * GN], start=True, stop=True)
                ins.then_inc(key_ready, 1)

            def weigh(u, way, s):
                c, j = STEPS[s]
                if j == 0:
                    if c == 0:
                        pe.wait_ge(v_loaded[way], (u - way) * (16 // WAYS) + 16)
                    at_least(pe, o_taken, 2 * u + c)
                if diagonal(s):
                    pe.wait_ge(masked, DIAGONAL * u + diagonals_to(s))
                else:
                    pe.wait_ge(weights_ready, 2 * (NSTEP * u + s + 1))
                for h in range(HG):
                    ins = nc.tensor.matmul(total[VW * h:VW * (h + 1), offset(s):GN], v[way][:, j, VW * h:VW * (h + 1)],
                                           e[s % E_RING][:, h, offset(s):GN], start=(j == 0), stop=(j == 4 * c + 3))
                ins.then_inc(summed, 1)

            def ahead(u, way, m):
                if m == TURN_AT and not is_first(u):
                    turn_rows(u - 1, (way - 1) % WAYS)
                if not (isinstance(u, int) and u >= UNITS):
                    piece(u, way, m)

            pe.wait_ge(consts, 3)
            for m in range(NP_UNIT):
                ahead(0, 0, m)
            for m in range(AHEAD):
                ahead(1, 1, m)
            pe.wait_ge(consts, 9)

            def step(u, way):
                order = [(u + 1, (way + 1) % WAYS, m) for m in range(AHEAD, NP_UNIT)] + [(u + 2, (way + 2) % WAYS, m) for m in range(AHEAD)]
                if is_last(u, UNITS):
                    order = []

                def pieces(n):
                    for at in order[SHARE[n]:SHARE[n + 1]]:
                        ahead(*at)
                for s in range(NSTEP):
                    scores(u, way, s, 0)
                    pieces(3 * s)
                    scores(u, way, s, 1)
                    pieces(3 * s + 1)
                    if s >= LAG:
                        weigh(u, way, s - LAG)
                    elif not is_first(u):
                        weigh(u - 1, (way - 1) % WAYS, NSTEP - LAG + s)
                    pieces(3 * s + 2)
            pipelined(pe, step, UNITS, WAYS)
            for s in range(NSTEP - LAG, NSTEP):
                weigh(UNITS - 1, WAYS - 1, s)


def attention_out(nc, x_in, o_in, w_o, x_out):
    with ExitStack() as ctx:
        sb = lambda n, s, d: ctx.enter_context(nc.sbuf_tensor(f"out_{n}", s, d))
        ps = lambda n, s, d=F32: ctx.enter_context(nc.psum_tensor(f"out_{n}", s, d))
        sem = lambda n: ctx.enter_context(nc.semaphore(f"out_{n}"))
        UG = HEADS // HG
        w_f = sb("w_f", [P, KC * D], F32)
        w_high = sb("w_high", [P, KC * D], F32R)
        w_low = sb("w_low", [P, KC * D], F32R)
        identity = sb("identity", [P, P], F32)
        o = [sb(f"o{i}", [P, UG, GN], F32) for i in range(2)]
        x = [sb(f"x{i}", [P, GT, D], F32) for i in range(2)]
        y = [sb(f"y{i}", [P, GT, D], F32) for i in range(2)]
        inverse = sb("inverse", [P, GT, HEADS], F32)
        merged = sb("merged", [P, GT, D], F32)
        high = sb("high", [P, KC, GN], F32R)
        low = sb("low", [P, KC, GN], F32R)
        sums = [ps(f"sums{i}", [P, UG * P]) for i in range(2)]
        turned = ps("turned", [P, KC, GN])
        out = ps("out", [P, GT, D])
        consts, w_loaded, w_ready = sem("consts"), sem("w_loaded"), sem("w_ready")
        loaded, x_loaded = [sem("loaded0"), sem("loaded1")], [sem("x_loaded0"), sem("x_loaded1")]
        sums_ready, inverse_ready, merged_ready = sem("sums_ready"), sem("inverse_ready"), sem("merged_ready")
        turned_ready, high_ready, low_ready, out_ready, y_ready = (sem(n) for n in ("turned_ready", "high_ready", "low_ready", "out_ready", "y_ready"))
        stored = [sem("stored0"), sem("stored1")]
        block = ctx.enter_context(nc.Block())

        @block.sync
        def _(sp):
            sp.dma_start(w_f[:].rearrange("p (c n) -> p c n", c=KC), w_o.rearrange("(c p) n -> p c n", p=P)).then_inc(w_loaded, 16)

            def load_o(g, slot, b):
                at_least(sp, sums_ready, GT * (g - 1))
                src = o_in[bass.ds(b * UG, UG), :, slot * GN:(slot + 1) * GN]
                sp.dma_start(o[slot][:], src.rearrange("u p n -> p u n")).then_inc(loaded[slot], 16)

            def load_x(g, slot):
                at_least(sp, y_ready, g - 1)
                sp.dma_start(x[slot][:], group_rows(x_in, g)).then_inc(x_loaded[slot], 16)

            def store(g, slot):
                sp.wait_ge(y_ready, g + 1)
                sp.dma_start(group_rows(x_out, g), y[slot][:]).then_inc(stored[slot], 16)

            def pair(b):
                for slot in range(2):
                    if not is_last(b, BATCH):
                        load_o(2 * b + 2 + slot, slot, b + 1)
                    if not (is_first(b) and slot == 0):
                        store(2 * b + slot - 1, 1 - slot)
                    if not (is_last(b, BATCH) and slot == 1):
                        load_x(2 * b + slot + 1, 1 - slot)
            load_o(0, 0, 0)
            load_o(1, 1, 0)
            load_x(0, 0)
            pair(0)
            with sp.Fori(1, BATCH - 1) as b:
                pair(b)
            pair(BATCH - 1)
            store(GROUPS - 1, 1)
            for s in stored:
                sp.wait_ge(s, 8 * GROUPS)

        @block.gpsimd
        def _(pool):
            fill_identity(nc, identity, consts)

        @block.scalar
        def _(act):
            def step(g, slot):
                act.wait_ge(turned_ready, g + 1)
                at_least(act, out_ready, g)
                nc.scalar.copy(high[:], turned[:]).then_inc(high_ready, 1)
            pipelined(act, step, GROUPS)

        @block.vector
        def _(dve):
            dve.wait_ge(w_loaded, 16)
            nc.vector.tensor_copy(w_high[:], w_f[:]).then_inc(w_ready, 1)
            dve.wait_ge(w_ready, 1)
            nc.vector.tensor_tensor(w_low[:], w_f[:], w_high[:].bitcast(F32), ALU.subtract).then_inc(w_ready, 1)

            def finish(g, slot):
                dve.wait_ge(out_ready, g + 1)
                dve.wait_ge(x_loaded[slot], 8 * g + 16 - 8 * slot)
                at_least(dve, stored[slot], 8 * g - 8 * slot)
                nc.vector.tensor_tensor(y[slot][:], out[:], x[slot][:], ALU.add).then_inc(y_ready, 1)

            def take_low(g):
                dve.wait_ge(high_ready, g + 1)
                nc.vector.tensor_tensor(low[:], turned[:], high[:].bitcast(F32), ALU.subtract).then_inc(low_ready, 1)

            def step(g, slot):
                if not is_first(g):
                    take_low(g - 1)
                at_least(dve, turned_ready, g)
                for t in range(GT):
                    n = GT * g + t
                    s = sums[t % 2][:].rearrange("p (h n) -> p h n", n=VW)
                    dve.wait_ge(sums_ready, n + 1)
                    nc.vector.reciprocal(inverse[:, t, :], s[:, :, HD]).then_inc(inverse_ready, 1)
                    dve.wait_ge(inverse_ready, n + 1)
                    nc.vector.tensor_tensor(merged[:, t, :].rearrange("p (h n) -> p h n", n=HD), s[:, :, 0:HD],
                                            inverse[:, t, :].unsqueeze(2).broadcast_to([P, HEADS, HD]), ALU.mult).then_inc(merged_ready, 1)
                if not is_first(g):
                    finish(g - 1, 1 - slot)
            pipelined(dve, step, GROUPS)
            take_low(GROUPS - 1)
            finish(GROUPS - 1, 1)

        @block.tensor
        def _(pe):
            pe.wait_ge(consts, 2)
            pe.wait_ge(w_ready, 2)

            def combine(g, t):
                if t == 0:
                    pe.wait_ge(low_ready, g + 1)
                    at_least(pe, y_ready, g)
                ts = slice(t * P, (t + 1) * P)
                ins = product(nc, out[:, t, :], [(high[:, c, ts], low[:, c, ts], w_high[:, c * D:(c + 1) * D], w_low[:, c * D:(c + 1) * D])
                                                 for c in range(KC)])
                if t == GT - 1:
                    ins.then_inc(out_ready, 1)

            def step(g, slot):
                pe.wait_ge(loaded[slot], 8 * g + 16 - 8 * slot)
                for t in range(GT):
                    n = GT * g + t
                    at_least(pe, merged_ready, n - 1)
                    for u in range(UG):
                        ins = nc.tensor.transpose(sums[t % 2][:, u * P:(u + 1) * P], o[slot][:, u, t * P:(t + 1) * P], identity[:])
                    ins.then_inc(sums_ready, 1)
                    if t >= 1 and not is_first(g):
                        combine(g - 1, t - 1)
                if not is_first(g):
                    combine(g - 1, GT - 1)
                pe.wait_ge(merged_ready, GT * (g + 1))
                for c in range(KC):
                    for t in range(GT):
                        ins = nc.tensor.transpose(turned[:, c, t * P:(t + 1) * P], merged[:, t, c * P:(c + 1) * P], identity[:])
                ins.then_inc(turned_ready, 1)
            pipelined(pe, step, GROUPS)
            for t in range(GT):
                combine(GROUPS - 1, t)
HIDDEN = 768
HC = HIDDEN // P
DEQUANT = float(np.float32(1.0 / 127.0))


def swiglu_ffn(nc, x_in, gate_up, down, x_out):
    with ExitStack() as ctx:
        sb = lambda n, s, d: ctx.enter_context(nc.sbuf_tensor(f"ffn_{n}", s, d))
        ps = lambda n, s: ctx.enter_context(nc.psum_tensor(f"ffn_{n}", s, F32))
        sem = lambda n: ctx.enter_context(nc.semaphore(f"ffn_{n}"))
        W1 = KC * 2 * HIDDEN
        W2 = HC * D
        PIECES_W = KC + 1
        WP = W1 // KC
        assert W2 == WP
        w_int = sb("w_int", [P, W1 + W2], I32)
        w_f = sb("w_f", [P, W1 + W2], F32)
        w_high = sb("w_high", [P, W1 + W2], F32R)
        w_low = sb("w_low", [P, W1 + W2], F32R)
        identity = sb("identity", [P, P], F32)
        ones = sb("ones", [P, P], F32)
        squares = sb("squares", [P, WP], F32)
        sizes = sb("sizes", [P, PIECES_W], F32)
        any_low = sb("any_low", [P, 1], F32)
        gated = [sb(f"gated{i}", [P, GN], F32) for i in range(2)]
        hidden = [sb(f"hidden{i}", [P, GN], F32) for i in range(2)]
        h_high = sb("h_high", [P, HC, GN], F32R)
        h_low = sb("h_low", [P, HC, GN], F32R)
        y = [sb(f"y{i}", [P, GT, D], F32) for i in range(2)]
        turned = ps("turned", [P, KC, GN])
        gate = [ps(f"gate{i}", [P, GN]) for i in range(2)]
        up = [ps(f"up{i}", [P, GN]) for i in range(2)]
        out = ps("out", [P, GT, D])
        f = Front(nc, ctx, "ffn", turned)
        w_loaded = [sem(f"w_loaded{i}") for i in range(PIECES_W)]
        w_float, w_high_ready, w_low_ready = sem("w_float"), sem("w_high_ready"), sem("w_low_ready")
        sizes_ready, sizes_summed, any_low_ready = sem("sizes_ready"), sem("sizes_summed"), sem("any_low_ready")
        identity_ready = sem("identity_ready")
        gate_ready, up_ready = sem("gate_ready"), sem("up_ready")
        gated_ready = sem("gated_ready")
        hidden_ready = sem("hidden_ready")
        h_high_ready, h_low_ready = sem("h_high_ready"), sem("h_low_ready")
        down_done = sem("down_done")
        y_ready = sem("y_ready")
        y_stored = [sem("y_stored_even"), sem("y_stored_odd")]

        def w1(column, c):
            s = slice(c * 2 * HIDDEN + column, c * 2 * HIDDEN + column + P)
            return w_high[:, s], w_low[:, s]

        def w2(c):
            s = slice(W1 + c * D, W1 + (c + 1) * D)
            return w_high[:, s], w_low[:, s]

        def piece(i):
            return slice(i * WP, (i + 1) * WP)

        block = ctx.enter_context(nc.Block())

        @block.sync
        def _(sp):
            f.load(x_in, 0, 0)
            for c in range(KC):
                sp.dma_start(w_int[:, piece(c)], gate_up[c * P:(c + 1) * P, :]).then_inc(w_loaded[c], 16)
            sp.dma_start(w_int[:, piece(KC)].rearrange("p (c n) -> p c n", c=HC),
                         down.rearrange("(c p) n -> p c n", p=P)).then_inc(w_loaded[KC], 16)
            f.load(x_in, 1, 1)

            def store(g, slot):
                sp.wait_ge(y_ready, g + 1)
                sp.dma_start(group_rows(x_out, g), y[slot][:]).then_inc(y_stored[slot], 16)

            def step(g, slot):
                if not (isinstance(g, int) and g + 2 >= GROUPS):
                    f.load(x_in, g + 2, slot)
                if not is_first(g):
                    store(g - 1, 1 - slot)
            pipelined(sp, step, GROUPS)
            store(GROUPS - 1, 1)
            for s in y_stored:
                sp.wait_ge(s, 8 * GROUPS)

        @block.gpsimd
        def _(pool):
            fill_identity(nc, identity, identity_ready)
            nc.gpsimd.memset(ones[:], 1.0).then_inc(identity_ready, 1)

            def step(g, slot):
                for c in range(HC):
                    n = g * HC + c
                    pool.wait_ge(h_high_ready, n + 1)
                    nc.gpsimd.tensor_tensor(h_low[:, c, :], hidden[c % 2][:], h_high[:, c, :].bitcast(F32),
                                            ALU.subtract).then_inc(h_low_ready, 1)
            pipelined(pool, step, GROUPS)

        @block.scalar
        def _(act):
            for i in range(PIECES_W):
                act.wait_ge(w_float, i + 1)
                nc.scalar.copy(w_high[:, piece(i)], w_f[:, piece(i)]).then_inc(w_high_ready, 1)
                if i == 0:
                    f.take_high(0, 0)
            for i in range(PIECES_W):
                act.wait_ge(w_low_ready, i + 1)
                at_least(act, sizes_ready, i)
                nc.scalar.activation(squares[:], w_low[:, piece(i)].bitcast(F32), ACT.Square,
                                     accum_out=sizes[:, i:i + 1]).then_inc(sizes_ready, 1)

            def take_hidden_high(n, c):
                act.wait_ge(hidden_ready, n + 1)
                at_least(act, down_done, n + 1 - HC)
                nc.scalar.copy(h_high[:, c, :], hidden[c % 2][:]).then_inc(h_high_ready, 1)

            def step(g, slot):
                for c in range(HC):
                    n = g * HC + c
                    act.wait_ge(gate_ready, n + 1)
                    at_least(act, hidden_ready, n - 1)
                    nc.scalar.activation(gated[c % 2][:], gate[c % 2][:], ACT.Silu, scale=DEQUANT).then_inc(gated_ready, 1)
                    if not (is_first(g) and c == 0):
                        take_hidden_high(n - 1, (c - 1) % HC)
                    if c == 4 and not is_last(g, GROUPS):
                        at_least(act, up_ready, HC * g)
                        f.take_high(g + 1, 1 - slot)
            pipelined(act, step, GROUPS)
            take_hidden_high(GROUPS * HC - 1, HC - 1)

        @block.vector
        def _(dve):
            f.normalise(0, 0)
            for i in range(PIECES_W):
                dve.wait_ge(w_loaded[i], 16)
                nc.vector.tensor_copy(w_f[:, piece(i)], w_int[:, piece(i)]).then_inc(w_float, 1)
            for i in range(PIECES_W):
                if i == 1:
                    f.take_low(0, 0)
                dve.wait_ge(w_high_ready, i + 1)
                nc.vector.tensor_tensor(w_low[:, piece(i)], w_f[:, piece(i)], w_high[:, piece(i)].bitcast(F32),
                                        ALU.subtract).then_inc(w_low_ready, 1)
            dve.wait_ge(sizes_summed, 1)
            nc.vector.reduce_sum(any_low[:], gate[0][:, 0:PIECES_W], AX_X).then_inc(any_low_ready, 1)

            def finish(g, slot):
                dve.wait_ge(down_done, HC * (g + 1))
                at_least(dve, y_stored[slot], 8 * g - 8 * slot)
                nc.vector.scalar_tensor_tensor(y[slot][:], out[:], DEQUANT, f.resid[slot][:], ALU.mult, ALU.add).then_inc(y_ready, 1)

            def step(g, slot):
                for c in range(HC):
                    n = g * HC + c
                    if c == 5 and not is_last(g, GROUPS):
                        f.take_low(g + 1, 1 - slot)
                    dve.wait_ge(gated_ready, n + 1)
                    dve.wait_ge(up_ready, n + 1)
                    at_least(dve, h_low_ready, n - 1)
                    nc.vector.scalar_tensor_tensor(hidden[c % 2][:], up[c % 2][:], DEQUANT, gated[c % 2][:], ALU.mult, ALU.mult).then_inc(hidden_ready, 1)
                    if c == 1 and not is_first(g):
                        finish(g - 1, 1 - slot)
                    if not is_last(g, GROUPS):
                        if c == 1:
                            f.take_moments(g + 1, 1 - slot, [(y_ready, g)])
                        if c == 2:
                            f.root(g + 1)
                        if c == 3:
                            f.scale(g + 1, 1 - slot)
            pipelined(dve, step, GROUPS)
            finish(GROUPS - 1, 1)

        @block.tensor
        def _(pe):
            pe.wait_ge(identity_ready, 3)
            f.turn(0, identity[:])
            pe.wait_ge(sizes_ready, PIECES_W)
            nc.tensor.matmul(gate[0][:, 0:PIECES_W], ones[:], sizes[:], start=True, stop=True).then_inc(sizes_summed, 1)

            def groups(low_halves):
                def down_chunk(n, c):
                    pe.wait_ge(h_low_ready, n + 1)
                    high, low = w2(c)
                    for t in range(GT):
                        ts = slice(t * P, (t + 1) * P)
                        ins = product(nc, out[:, t, :], [(h_high[:, c, ts], h_low[:, c, ts], high, low if low_halves else None)],
                                      start=(c == 0 and t % 2 == 0), stop=(c == HC - 1), shared=True)
                    ins.then_inc(down_done, 1)

                def step(g, slot):
                    pe.wait_ge(f.low_ready, g + 1)
                    for c in range(HC):
                        n = g * HC + c
                        at_least(pe, hidden_ready, n - 1)
                        for bank, base, ready in ((gate, 0, gate_ready), (up, HIDDEN, up_ready)):
                            pairs = []
                            for k in range(KC):
                                high, low = w1(base + c * P, k)
                                pairs.append((high, low if low_halves else None, f.high[slot][:, k, :], f.low[slot][:, k, :]))
                            product(nc, bank[c % 2][:], pairs).then_inc(ready, 1)
                        if c >= 2:
                            if c == 2:
                                at_least(pe, y_ready, g)
                            down_chunk(n - 2, c - 2)
                        elif not is_first(g):
                            down_chunk(n - 2, HC - 2 + c)
                        if c == 4 and not is_last(g, GROUPS):
                            f.turn(g + 1, identity[:])
                pipelined(pe, step, GROUPS)
                down_chunk(GROUPS * HC - 2, HC - 2)
                down_chunk(GROUPS * HC - 1, HC - 1)

            pe.wait_ge(any_low_ready, 1)
            bits = pe.value_load(any_low[0:1, 0:1].bitcast(I32))
            with pe.If(bits != 0):
                groups(True)
            with pe.Else():
                groups(False)
SCORE_SCALE = float(D) ** -0.5


def column_attention(nc, x_in, w_qkv, x_out):
    with ExitStack() as ctx:
        sb = lambda n, s, d: ctx.enter_context(nc.sbuf_tensor(f"col_{n}", s, d))
        ps = lambda n, s, d=F32: ctx.enter_context(nc.psum_tensor(f"col_{n}", s, d))
        sem = lambda n: ctx.enter_context(nc.semaphore(f"col_{n}"))
        W = KC * 3 * D
        NB = SEQ // P
        BLOCKS = BATCH * NB
        FILLS = 12
        w_f = sb("w_f", [P, W], F32)
        w_high = sb("w_high", [P, W], F32R)
        w_low = sb("w_low", [P, W], F32R)
        identity = sb("identity", [P, P], F32)
        qk_high = sb("qk_high", [P, 2 * KC, SEQ], F32R)
        qk_low = sb("qk_low", [P, 2 * KC, SEQ], F32R)
        v_high = sb("v_high", [P, NB, D], F32R)
        v_low = sb("v_low", [P, NB, D], F32R)
        weights = [sb(f"weights{i}", [P, SEQ], F32) for i in range(2)]
        t_high = [sb(f"t_high{i}", [P, NB, P], F32R) for i in range(2)]
        t_low = [sb(f"t_low{i}", [P, NB, P], F32R) for i in range(2)]
        top = sb("top", [P, 4], F32)
        bias = sb("bias", [P, 4], F32)
        total = sb("total", [P, 4], F32)
        inverse = sb("inverse", [P, 4], F32)
        x = [sb(f"xb{i}", [P, D], F32) for i in range(2)]
        y = [sb(f"y{i}", [P, D], F32) for i in range(2)]
        turned = ps("turned", [P, KC, GN])
        scores = [ps(f"scores{i}", [P, SEQ]) for i in range(2)]
        out = [ps(f"out{i}", [P, GN]) for i in range(2)]
        f = Front(nc, ctx, "col", turned)
        consts, w_loaded, w_ready = sem("consts"), sem("w_loaded"), sem("w_ready")
        fill_ready, fill_high, fill_low = sem("fill_ready"), sem("fill_high"), sem("fill_low")
        scores_ready = sem("scores_ready")
        top_ready, bias_ready = sem("top_ready"), sem("bias_ready")
        weights_ready = sem("weights_ready")
        t_turned, t_high_ready, t_low_ready = sem("t_turned"), sem("t_high_ready"), sem("t_low_ready")
        out_ready = sem("out_ready")
        inverse_ready, y_ready = sem("inverse_ready"), sem("y_ready")
        xb_loaded = [sem("xb_loaded0"), sem("xb_loaded1")]
        stored = [sem("stored0"), sem("stored1")]
        block = ctx.enter_context(nc.Block())

        def bank(i):
            return scores[i // 2][:, (i % 2) * GN:(i % 2 + 1) * GN]

        def fill_target(i, lo):
            if i < 8:
                a = qk_low if lo else qk_high
                return a[:, i % 4, (i // 4) * GN:(i // 4 + 1) * GN]
            a = v_low if lo else v_high
            return a[:, 2 * (i - 8):2 * (i - 8) + 2, :].rearrange("p t n -> p (t n)")

        def rows(ap, n):
            return ap[bass.ds(n * P, P), :]

        def batches(engine, step):
            step(0)
            with engine.Fori(1, BATCH - 1) as b:
                step(b)
            step(BATCH - 1)

        FRONT_AT = {3: 0, 6: 1}

        @block.sync
        def _(sp):
            f.load(x_in, 0, 0)
            sp.dma_start(w_f[:].rearrange("p (c n) -> p c n", c=KC), w_qkv.rearrange("(c p) n -> p c n", p=P)).then_inc(w_loaded, 16)
            f.load(x_in, 1, 1)

            def store(n, slot):
                sp.wait_ge(y_ready, n + 1)
                sp.dma_start(rows(x_out, n), y[slot][:]).then_inc(stored[slot], 16)

            def step(b):
                if not is_last(b, BATCH):
                    f.load(x_in, 2 * b + 2, 0)
                    f.load(x_in, 2 * b + 3, 1)
                for j in range(NB):
                    n = NB * b + j
                    if j >= 2 or not is_first(b):
                        store(n - 2, j % 2)
                    sp.dma_start(x[j % 2][:], rows(x_in, n)).then_inc(xb_loaded[j % 2], 16)
            batches(sp, step)
            store(BLOCKS - 2, 0)
            store(BLOCKS - 1, 1)
            for s in stored:
                sp.wait_ge(s, 8 * BLOCKS)

        @block.gpsimd
        def _(pool):
            fill_identity(nc, identity, consts)

        @block.scalar
        def _(act):
            f.take_high(0, 0)

            def high(n, slot):
                act.wait_ge(t_turned, n + 1)
                at_least(act, out_ready, n - 1)
                nc.scalar.copy(t_high[slot][:], turned[:].rearrange("p c (t n) -> p (c t) n", n=P)).then_inc(t_high_ready, 1)

            def step(b):
                for i in range(FILLS):
                    if i == 4 and not is_first(b):
                        high(NB * b - 1, 1)
                    act.wait_ge(fill_ready, FILLS * b + i + 1)
                    nc.scalar.copy(fill_target(i, False), bank(i % 4)).then_inc(fill_high, 1)
                    if i == 1 and is_first(b):
                        f.take_high(1, 1)
                for j in range(NB):
                    n = NB * b + j
                    if j in FRONT_AT and not is_last(b, BATCH):
                        f.take_high(2 * b + 2 + FRONT_AT[j], FRONT_AT[j])
                    if j == 1:
                        high(n - 1, 0)
                    act.wait_ge(bias_ready, n + 1)
                    at_least(act, t_turned, n - 1)
                    nc.scalar.activation(weights[j % 2][:], scores[j % 2][:], ACT.Exp, bias=bias[:, j % 4:j % 4 + 1],
                                         scale=SCORE_SCALE, accum_out=total[:, j % 4:j % 4 + 1]).then_inc(weights_ready, 1)
                    if j > 1:
                        high(n - 1, (j - 1) % 2)
            batches(act, step)
            high(BLOCKS - 1, 1)

        @block.vector
        def _(dve):
            f.normalise(0, 0, keep=False)
            dve.wait_ge(w_loaded, 16)
            nc.vector.tensor_copy(w_high[:], w_f[:]).then_inc(w_ready, 1)
            dve.wait_ge(w_ready, 1)
            nc.vector.tensor_tensor(w_low[:], w_f[:], w_high[:].bitcast(F32), ALU.subtract).then_inc(w_ready, 1)
            f.take_low(0, 0)
            f.normalise(1, 1, keep=False)

            def low(n, slot):
                dve.wait_ge(t_high_ready, n + 1)
                nc.vector.tensor_tensor(t_low[slot][:], turned[:].rearrange("p c (t n) -> p (c t) n", n=P),
                                        t_high[slot][:].bitcast(F32), ALU.subtract).then_inc(t_low_ready, 1)

            def finish(n, j):
                dve.wait_ge(out_ready, n + 1)
                nc.vector.reciprocal(inverse[:, j % 4:j % 4 + 1], total[:, j % 4:j % 4 + 1]).then_inc(inverse_ready, 1)
                dve.wait_ge(xb_loaded[j % 2], 8 * (n - j % 2) + 16)
                at_least(dve, stored[j % 2], 8 * (n - j % 2))
                dve.wait_ge(inverse_ready, n + 1)
                nc.vector.scalar_tensor_tensor(y[j % 2][:], out[j % 2][:, 0:D], inverse[:, j % 4:j % 4 + 1], x[j % 2][:],
                                               ALU.mult, ALU.add).then_inc(y_ready, 1)

            def step(b):
                for i in range(FILLS):
                    if not is_first(b):
                        if i == 4:
                            low(NB * b - 1, 1)
                            finish(NB * b - 2, NB - 2)
                        if i == 8:
                            finish(NB * b - 1, NB - 1)
                    dve.wait_ge(fill_high, FILLS * b + i + 1)
                    nc.vector.tensor_tensor(fill_target(i, True), bank(i % 4), fill_target(i, False).bitcast(F32),
                                            ALU.subtract).then_inc(fill_low, 1)
                    if i == 1 and is_first(b):
                        f.take_low(1, 1)
                for j in range(NB):
                    n = NB * b + j
                    dve.wait_ge(scores_ready, n + 1)
                    nc.vector.reduce_max(top[:, j % 4:j % 4 + 1], scores[j % 2][:], AX_X).then_inc(top_ready, 1)
                    dve.wait_ge(top_ready, n + 1)
                    nc.vector.tensor_scalar(bias[:, j % 4:j % 4 + 1], top[:, j % 4:j % 4 + 1], -SCORE_SCALE, None, ALU.mult).then_inc(bias_ready, 1)
                    if j in FRONT_AT and not is_last(b, BATCH):
                        f.take_low(2 * b + 2 + FRONT_AT[j], FRONT_AT[j])
                    if not is_last(b, BATCH):
                        if j + 3 in FRONT_AT:
                            f.take_moments(2 * b + 2 + FRONT_AT[j + 3], FRONT_AT[j + 3], keep=False)
                        if j + 2 in FRONT_AT:
                            f.root(2 * b + 2 + FRONT_AT[j + 2])
                        if j + 1 in FRONT_AT:
                            f.scale(2 * b + 2 + FRONT_AT[j + 1], FRONT_AT[j + 1])
                    if j >= 1:
                        low(n - 1, (j - 1) % 2)
                    if j >= 2:
                        finish(n - 2, j - 2)
            batches(dve, step)
            low(BLOCKS - 1, 1)
            finish(BLOCKS - 2, NB - 2)
            finish(BLOCKS - 1, NB - 1)

        @block.tensor
        def _(pe):
            pe.wait_ge(consts, 2)
            f.turn(0, identity[:])
            pe.wait_ge(w_ready, 2)

            def w(c, column, width):
                s = slice(c * 3 * D + column, c * 3 * D + column + width)
                return w_high[:, s], w_low[:, s]

            def fill(b, i):
                if i == 0:
                    pe.wait_ge(f.low_ready, 2 * b + 1)
                if i == 4:
                    pe.wait_ge(f.low_ready, 2 * b + 2)
                if i < 4:
                    at_least(pe, weights_ready, NB * b)
                    at_least(pe, fill_low, FILLS * b)
                else:
                    pe.wait_ge(fill_low, FILLS * b + i - 3)
                if i < 8:
                    slot = i // 4
                    ins = product(nc, bank(i % 4), [(*w(c, (i % 4) * P, P), f.high[slot][:, c, :], f.low[slot][:, c, :]) for c in range(KC)])
                else:
                    for half in range(2):
                        t = 2 * (i - 8) + half
                        slot, ts = t // GT, slice((t % GT) * P, (t % GT + 1) * P)
                        ins = product(nc, bank(i % 4)[:, half * D:(half + 1) * D],
                                      [(f.high[slot][:, c, ts], f.low[slot][:, c, ts], *w(c, 2 * D, D)) for c in range(KC)])
                ins.then_inc(fill_ready, 1)

            def turn(n, slot):
                pe.wait_ge(weights_ready, n + 1)
                at_least(pe, t_low_ready, n)
                for c in range(NB):
                    ins = nc.tensor.transpose(turned[:, c // GT, (c % GT) * P:(c % GT + 1) * P], weights[slot][:, c * P:(c + 1) * P], identity[:])
                ins.then_inc(t_turned, 1)

            def weigh(n, slot):
                pe.wait_ge(t_low_ready, n + 1)
                at_least(pe, y_ready, n - 1)
                product(nc, out[slot][:, 0:D], [(t_high[slot][:, c, :], t_low[slot][:, c, :], v_high[:, c, :], v_low[:, c, :])
                                                for c in range(NB)]).then_inc(out_ready, 1)

            def step(b):
                for i in range(FILLS):
                    if not is_first(b):
                        if i == 4:
                            turn(NB * b - 1, 1)
                            weigh(NB * b - 2, 0)
                        if i == 8:
                            weigh(NB * b - 1, 1)
                    fill(b, i)
                    if i == 1 and is_first(b):
                        f.turn(1, identity[:])
                for j in range(NB):
                    n = NB * b + j
                    if j < 2:
                        pe.wait_ge(fill_low, FILLS * (b + 1) - 2 + 2 * j)
                    if j >= 2:
                        pe.wait_ge(weights_ready, n - 1)
                    for half in range(2):
                        hs, js = slice(half * GN, (half + 1) * GN), slice(j * P, (j + 1) * P)
                        ins = product(nc, scores[j % 2][:, hs], [(qk_high[:, KC + c, js], qk_low[:, KC + c, js], qk_high[:, c, hs], qk_low[:, c, hs])
                                                                 for c in range(KC)])
                    ins.then_inc(scores_ready, 1)
                    if j in FRONT_AT and not is_last(b, BATCH):
                        pe.wait_ge(t_low_ready, n - 1)
                        f.turn(2 * b + 2 + FRONT_AT[j], identity[:])
                        weigh(n - 2, j % 2)
                        pe.wait_ge(f.low_ready, 2 * b + 3 + FRONT_AT[j])
                        turn(n - 1, (j - 1) % 2)
                    else:
                        if j >= 1:
                            turn(n - 1, (j - 1) % 2)
                        if j >= 2:
                            weigh(n - 2, j % 2)
            batches(pe, step)
            turn(BLOCKS - 1, 1)
            weigh(BLOCKS - 2, 0)
            weigh(BLOCKS - 1, 1)
EXPERTS = 16
CHUNKS = EXPERTS + 2


class Router:

    STEPS = 11 + 2 * GT

    def __init__(self, nc, ctx, logits):
        sb = lambda n, s, d=F32: ctx.enter_context(nc.sbuf_tensor(f"router_{n}", s, d))
        sem = lambda n: ctx.enter_context(nc.semaphore(f"router_{n}"))
        self.nc, self.logits = nc, logits
        self.wide = [P, GT, EXPERTS]
        self.centred, self.e, self.p, self.hit, self.hit1 = (sb(n, [P, GT, EXPERTS]) for n in ("centred", "e", "p", "hit", "hit1"))
        self.cw = [sb(f"cw{i}", [P, GT, EXPERTS]) for i in range(2)]
        self.top, self.total, self.inverse = (sb(n, [P, GT]) for n in ("top", "total", "inverse"))
        self.best = sb("best", [P, GT, 8])
        self.where, self.where_f = sb("where", [P, GT, 8], U32), sb("where_f", [P, GT, 8])
        self.number = sb("number", [P, EXPERTS])
        self.logits_ready, self.chain, self.e_ready = sem("logits_ready"), sem("chain"), sem("e_ready")

    def chained(self, g, done, ops):
        for n, op in enumerate(ops):
            op().then_inc(self.chain, 1)
            waits_apart(self.nc.vector, (self.chain, self.STEPS * g + done + n + 1))

    def centre(self, g):
        dve = self.nc.vector
        l = self.logits.rearrange("p (t e) -> p t e", e=EXPERTS)
        dve.wait_ge(self.logits_ready, g + 1)
        self.chained(g, 0, [lambda: dve.reduce_max(self.top[:], l, AX_X),
                            lambda: dve.tensor_tensor(self.centred[:], l, self.over(self.top[:]), ALU.subtract)])

    def find(self, g):
        dve = self.nc.vector
        dve.wait_ge(self.e_ready, g + 1)
        self.chained(g, 2, [lambda: dve.reduce_sum(self.total[:], self.e[:], AX_X),
                            lambda: dve.reciprocal(self.inverse[:], self.total[:]),
                            lambda: dve.tensor_tensor(self.p[:], self.e[:], self.over(self.inverse[:]), ALU.mult)])
        for t in range(GT):
            dve.max(self.best[:, t, :], self.p[:, t, :]).then_inc(self.chain, 1)
        waits_apart(dve, (self.chain, self.STEPS * g + 5 + GT))
        for t in range(GT):
            dve.max_index(self.where[:, t, :], self.best[:, t, :], self.p[:, t, :]).then_inc(self.chain, 1)
        waits_apart(dve, (self.chain, self.STEPS * g + 5 + 2 * GT))
        self.chained(g, 5 + 2 * GT, [lambda: dve.tensor_copy(self.where_f[:], self.where[:])])

    def weigh(self, g, slot):
        dve = self.nc.vector
        number = self.number[:].unsqueeze(1).broadcast_to(self.wide)
        self.chained(g, 6 + 2 * GT, [
            lambda: dve.tensor_tensor(self.hit[:], number, self.over(self.where_f[:, :, 0]), ALU.is_equal),
            lambda: dve.tensor_tensor(self.hit1[:], number, self.over(self.where_f[:, :, 1]), ALU.is_equal),
            lambda: dve.tensor_tensor(self.hit[:], self.hit[:], self.over(self.best[:, :, 0]), ALU.mult),
            lambda: dve.tensor_tensor(self.hit1[:], self.hit1[:], self.over(self.best[:, :, 1]), ALU.mult),
            lambda: dve.tensor_tensor(self.cw[slot][:], self.hit[:], self.hit1[:], ALU.add)])

    def over(self, a):
        return a.unsqueeze(2).broadcast_to(self.wide)

    def exponentials(self, g):
        act = self.nc.scalar
        act.wait_ge(self.chain, self.STEPS * g + 2)
        act.activation(self.e[:], self.centred[:], ACT.Exp).then_inc(self.e_ready, 1)


def experts(nc, x_in, w_router, gate_up, down, x_out):
    with ExitStack() as ctx:
        sb = lambda n, s, d: ctx.enter_context(nc.sbuf_tensor(f"moe_{n}", s, d))
        ps = lambda n, s: ctx.enter_context(nc.psum_tensor(f"moe_{n}", s, F32))
        sem = lambda n: ctx.enter_context(nc.semaphore(f"moe_{n}"))
        WC = KC * 2 * P + D
        W = CHUNKS * WC
        RING = 3
        HC = CHUNKS
        w_f = [sb(f"w_f{i}", [P, WC], F32) for i in range(2)]
        w_high = sb("w_high", [P, W], F32R)
        w_low = sb("w_low", [P, W], F32R)
        r_f = sb("r_f", [P, KC * EXPERTS], F32)
        r_high = sb("r_high", [P, KC * EXPERTS], F32R)
        r_low = sb("r_low", [P, KC * EXPERTS], F32R)
        identity = sb("identity", [P, P], F32)
        gated = [sb(f"gated{i}", [P, GN], F32) for i in range(2)]
        hidden = [sb(f"hidden{i}", [P, GN], F32) for i in range(2)]
        h_high = sb("h_high", [P, RING, GN], F32R)
        h_low = sb("h_low", [P, RING, GN], F32R)
        turned = ps("turned", [P, KC, GN])
        gate = [ps(f"gate{i}", [P, GN]) for i in range(2)]
        up = [ps(f"up{i}", [P, GN]) for i in range(2)]
        out = ps("out", [P, GT, D])
        f = Front(nc, ctx, "moe", turned)
        router = Router(nc, ctx, turned[:, 0, 0:GT * EXPERTS])
        w_loaded, w_split, w_ready, consts = [sem("w_loaded0"), sem("w_loaded1")], sem("w_split"), sem("w_ready"), sem("consts")
        r_loaded = sem("r_loaded")
        gate_ready, up_ready, gated_ready, hidden_ready = (sem(n) for n in ("gate_ready", "up_ready", "gated_ready", "hidden_ready"))
        h_high_ready, h_low_ready, down_done, out_read = (sem(n) for n in ("h_high_ready", "h_low_ready", "down_done", "out_read"))
        y_ready = sem("y_ready")
        y_stored = [sem("y_stored0"), sem("y_stored1")]

        def w1(c, kind, k):
            s = slice(c * WC + k * 2 * P + kind * P, c * WC + k * 2 * P + kind * P + P)
            return w_high[:, s], w_low[:, s]

        def w2(c):
            s = slice(c * WC + KC * 2 * P, (c + 1) * WC)
            return w_high[:, s], w_low[:, s]

        block = ctx.enter_context(nc.Block())

        @block.sync
        def _(sp):
            f.load(x_in, 0, 0)
            sp.dma_start(r_f[:].rearrange("p (c n) -> p c n", c=KC), w_router.rearrange("(c p) n -> p c n", p=P)).then_inc(r_loaded, 16)
            f.load(x_in, 1, 1)
            for c in range(CHUNKS):
                at_least(sp, w_split, 2 * c if c >= 2 else 0)
                sp.dma_start(w_f[c % 2][:, 0:KC * 2 * P].rearrange("p (c n) -> p c n", c=KC), gate_up[c].rearrange("(c p) n -> p c n", p=P)).then_inc(w_loaded[c % 2], 16)
                sp.dma_start(w_f[c % 2][:, KC * 2 * P:WC], down[c * P:(c + 1) * P, :]).then_inc(w_loaded[c % 2], 16)

            def store(g, slot):
                sp.wait_ge(y_ready, g + 1)
                sp.dma_start(group_rows(x_out, g), f.resid[slot][:]).then_inc(y_stored[slot], 16)

            def step(g, slot):
                if not (isinstance(g, int) and g + 2 >= GROUPS):
                    f.load(x_in, g + 2, slot)
                if not is_first(g):
                    store(g - 1, 1 - slot)
            pipelined(sp, step, GROUPS)
            store(GROUPS - 1, 1)
            for s in y_stored:
                sp.wait_ge(s, 8 * GROUPS)

        @block.gpsimd
        def _(pool):
            fill_identity(nc, identity, consts)
            nc.gpsimd.iota(router.number[:], [[1, EXPERTS]], base=0, channel_multiplier=0,
                           allow_small_or_imprecise_dtypes=True).then_inc(consts, 1)

            def step(g, slot):
                for c in range(HC):
                    n = g * HC + c
                    pool.wait_ge(h_high_ready, n + 1)
                    nc.gpsimd.tensor_tensor(h_low[:, c % RING, :], hidden[c % 2][:], h_high[:, c % RING, :].bitcast(F32),
                                            ALU.subtract).then_inc(h_low_ready, 1)
            pipelined(pool, step, GROUPS)

        @block.scalar
        def _(act):
            f.take_high(0, 0)
            router.exponentials(0)

            def take_hidden_high(n, at, ring):
                act.wait_ge(hidden_ready, n + 1)
                at_least(act, down_done, n + 1 - RING)
                nc.scalar.copy(h_high[:, ring, :], hidden[at][:]).then_inc(h_high_ready, 1)

            def step(g, slot):
                for c in range(HC):
                    n = g * HC + c
                    act.wait_ge(gate_ready, n + 1)
                    at_least(act, hidden_ready, n - 1)
                    nc.scalar.activation(gated[c % 2][:], gate[c % 2][:], ACT.Silu).then_inc(gated_ready, 1)
                    if not (is_first(g) and c == 0):
                        take_hidden_high(n - 1, (c - 1) % 2, (c - 1) % RING)
                    if c == 7 and not is_last(g, GROUPS):
                        at_least(act, up_ready, HC * g)
                        f.take_high(g + 1, 1 - slot)
                    if c == 11 and not is_last(g, GROUPS):
                        router.exponentials(g + 1)
            pipelined(act, step, GROUPS)
            take_hidden_high(GROUPS * HC - 1, (HC - 1) % 2, (HC - 1) % RING)

        @block.vector
        def _(dve):
            f.normalise(0, 0)
            dve.wait_ge(r_loaded, 16)
            dve.wait_ge(consts, 3)
            nc.vector.tensor_copy(r_high[:], r_f[:]).then_inc(w_split, 1)
            dve.wait_ge(w_split, 1)
            nc.vector.tensor_tensor(r_low[:], r_f[:], r_high[:].bitcast(F32), ALU.subtract).then_inc(w_split, 1)
            f.take_low(0, 0)

            def split_weights(c):
                s = slice(c * WC, (c + 1) * WC)
                dve.wait_ge(w_loaded[c % 2], 32 * (c // 2 + 1))
                nc.vector.tensor_copy(w_high[:, s], w_f[c % 2][:]).then_inc(w_split, 1)
                dve.wait_ge(w_split, 2 * c + 3)
                nc.vector.tensor_tensor(w_low[:, s], w_f[c % 2][:], w_high[:, s].bitcast(F32), ALU.subtract).then_inc(w_split, 1)
            split_weights(0)
            router.centre(0)
            split_weights(1)
            router.find(0)
            router.weigh(0, 0)

            def collect(g, slot, c):
                n = HC * g + c
                if c == EXPERTS:
                    return
                waits_apart(dve, (down_done, n + 1), (out_read, EXPERTS * g + min(c, EXPERTS)))
                if c == CHUNKS - 1:
                    nc.vector.tensor_tensor(f.resid[slot][:], f.resid[slot][:], out[:], ALU.add).then_inc(y_ready, 1)
                    return
                for t in range(GT):
                    ins = nc.vector.scalar_tensor_tensor(f.resid[slot][:, t, :], out[:, t, :], router.cw[slot][:, t, c:c + 1], f.resid[slot][:, t, :],
                                                         ALU.mult, ALU.add)
                ins.then_inc(out_read, 1)

            def step(g, slot):
                for c in range(HC):
                    n = g * HC + c
                    dve.wait_ge(gated_ready, n + 1)
                    dve.wait_ge(up_ready, n + 1)
                    at_least(dve, h_low_ready, n - 1)
                    nc.vector.tensor_tensor(hidden[c % 2][:], gated[c % 2][:], up[c % 2][:], ALU.mult).then_inc(hidden_ready, 1)
                    if c >= 2:
                        collect(g, slot, c - 2)
                    elif not is_first(g):
                        collect(g - 1, 1 - slot, HC - 2 + c)
                    if not is_last(g, GROUPS):
                        if c == 2:
                            f.take_moments(g + 1, 1 - slot, [(y_ready, g), (y_stored[1 - slot], 8 * (g + slot))])
                        if c == 3:
                            f.root(g + 1)
                        if c == 4:
                            f.scale(g + 1, 1 - slot)
                        if c == 8:
                            f.take_low(g + 1, 1 - slot)
                    if is_first(g) and c + 2 < CHUNKS:
                        split_weights(c + 2)
                    if not is_last(g, GROUPS):
                        if c == 10:
                            router.centre(g + 1)
                        if c == 12:
                            router.find(g + 1)
                        if c == 14:
                            router.weigh(g + 1, 1 - slot)
            pipelined(dve, step, GROUPS)
            collect(GROUPS - 1, 1, HC - 2)
            collect(GROUPS - 1, 1, HC - 1)

        @block.tensor
        def _(pe):
            pe.wait_ge(consts, 2)
            f.turn(0, identity[:])

            def down_chunk(g, c):
                n = HC * g + c
                pe.wait_ge(h_low_ready, n + 1)
                if c == 0:
                    at_least(pe, y_ready, g)
                elif c <= EXPERTS:
                    pe.wait_ge(out_read, EXPERTS * g + c)
                for t in range(GT):
                    ts = slice(t * P, (t + 1) * P)
                    ins = product(nc, out[:, t, :], [(h_high[:, c % RING, ts], h_low[:, c % RING, ts], *w2(c))],
                                  start=(c <= EXPERTS and t % 2 == 0), stop=(c != EXPERTS), shared=True)
                ins.then_inc(down_done, 1)

            def route(g, slot):
                pe.wait_ge(f.low_ready, g + 1)
                for t in range(GT):
                    ts = slice(t * P, (t + 1) * P)
                    ins = product(nc, turned[:, 0, t * EXPERTS:(t + 1) * EXPERTS],
                                  [(f.high[slot][:, k, ts], f.low[slot][:, k, ts], r_high[:, k * EXPERTS:(k + 1) * EXPERTS], r_low[:, k * EXPERTS:(k + 1) * EXPERTS])
                                   for k in range(KC)])
                ins.then_inc(router.logits_ready, 1)
            pe.wait_ge(w_split, 2)
            route(0, 0)

            def step(g, slot):
                for c in range(HC):
                    n = g * HC + c
                    if is_first(g):
                        pe.wait_ge(w_split, 2 * c + 4)
                    at_least(pe, hidden_ready, n - 1)
                    for bank, kind, ready in ((gate, 0, gate_ready), (up, 1, up_ready)):
                        product(nc, bank[c % 2][:], [(*w1(c, kind, k), f.high[slot][:, k, :], f.low[slot][:, k, :])
                                                     for k in range(KC)]).then_inc(ready, 1)
                    if c >= 2:
                        down_chunk(g, c - 2)
                    elif not is_first(g):
                        down_chunk(g - 1, HC - 2 + c)
                    if c == 9 and not is_last(g, GROUPS):
                        route(g + 1, 1 - slot)
                    if c == 6 and not is_last(g, GROUPS):
                        pe.wait_ge(router.chain, Router.STEPS * g + 2)
                        f.turn(g + 1, identity[:])
            pipelined(pe, step, GROUPS)
            down_chunk(GROUPS - 1, HC - 2)
            down_chunk(GROUPS - 1, HC - 1)


def rope_tables():
    f = (1.0 / 10000.0 ** (np.arange(0, HD, 2, dtype=np.float32) / HD)).astype(np.float32)
    a = np.arange(SEQ, dtype=np.float32)[:, None] * f[None, :]
    return np.cos(a).astype(np.float32), np.concatenate([-np.sin(a), np.sin(a)], axis=1).astype(np.float32)


def even_first(w):
    return w.reshape(D, HEADS, HALF, 2).transpose(0, 1, 3, 2).reshape(D, D)


def build(nc, inputs, out):
    scratch = lambda n, s, d=F32: nc.dram_tensor(n, s, d, kind="Internal").ap()
    qk = scratch("qk", (UNITS, QK * PARTS, HG * HD, SEQ), BF16)
    v = scratch("v", (UNITS, SEQ, HG * VW))
    att = scratch("att", (UNITS, P, SEQ))
    x1, x2, x3 = (scratch(f"x{i}", (TOKENS, D)) for i in (1, 2, 3))
    rope_qkv(nc, inputs["x"], inputs["w_qkv0"], inputs["cos"], inputs["sin"], qk, v)
    causal_attention(nc, qk, v, att)
    attention_out(nc, inputs["x"], att, inputs["w_o"], x1)
    swiglu_ffn(nc, x1, inputs["gate_up0"], inputs["down0"], x2)
    column_attention(nc, x2, inputs["w_qkv1"], x3)
    experts(nc, x3, inputs["w_router"], inputs["gate_up1"], inputs["down1"], out)


def kernel(L0_attn_x, L0_attn_qw, L0_attn_kw, L0_attn_vw, L0_attn_ow, L0_ffn_w_gate, L0_ffn_w_up, L0_ffn_w_down,
           L1_attn_W_query, L1_attn_W_key, L1_attn_W_value, L1_ffn_Wr, L1_ffn_Wg, L1_ffn_Wu, L1_ffn_Wd,
           L1_ffn_Sg, L1_ffn_Su, L1_ffn_Sd):
    import concourse.bacc as bacc
    from concourse.bass_utils import run_bass_kernel_spmd

    cat = lambda *a, axis: np.ascontiguousarray(np.concatenate(a, axis=axis))
    cos, sin = rope_tables()
    chunked = lambda w: w.reshape(D, 2, P).transpose(1, 0, 2)
    arrays = {
        "x": np.ascontiguousarray(L0_attn_x).reshape(TOKENS, D),
        "w_qkv0": cat(even_first(L0_attn_qw), even_first(L0_attn_kw), L0_attn_vw, axis=1),
        "cos": cos, "sin": sin,
        "w_o": np.ascontiguousarray(L0_attn_ow),
        "gate_up0": cat(L0_ffn_w_gate.T, L0_ffn_w_up.T, axis=1),
        "down0": np.ascontiguousarray(L0_ffn_w_down.T),
        "w_qkv1": cat(L1_attn_W_query, L1_attn_W_key, L1_attn_W_value, axis=1),
        "w_router": np.ascontiguousarray(L1_ffn_Wr),
        "gate_up1": cat(cat(L1_ffn_Wg, L1_ffn_Wu, axis=2), cat(chunked(L1_ffn_Sg), chunked(L1_ffn_Su), axis=2), axis=0),
        "down1": cat(L1_ffn_Wd.reshape(EXPERTS * P, D), L1_ffn_Sd, axis=0),
    }
    nc = bacc.Bacc("TRN2", target_bir_lowering=False, num_devices=1)
    inputs = {n: nc.dram_tensor(n, a.shape, mybir.dt.from_np(a.dtype), kind="ExternalInput").ap() for n, a in arrays.items()}
    out = nc.dram_tensor("out", (TOKENS, D), F32, kind="ExternalOutput").ap()
    build(nc, inputs, out)
    result = run_bass_kernel_spmd(nc, [arrays], core_ids=[0])
    return result.results[0]["out"].reshape(BATCH, SEQ, D)
```
